# Optimizing a Trainium2 kernel written in Bass

```python
import numpy as np
import jax
import jax.numpy as jnp

def _softmax(x, axis=-1):
    return jax.nn.softmax(x, axis=axis)

def _gelu(x):
    return jax.nn.gelu(x, approximate=True)

def _silu(x):
    return jax.nn.silu(x)

def _sigmoid(x):
    return jax.nn.sigmoid(x)

def _layernorm(x, axis=-1, eps=1e-05):
    m = jnp.mean(x, axis=axis, keepdims=True)
    v = jnp.var(x, axis=axis, keepdims=True)
    return (x - m) / jnp.sqrt(v + eps)

def _scatter_add(tgt, idx, src, axis=0):
    return tgt.at[idx].add(src)

def _segment_sum(src, seg, n):
    return jax.ops.segment_sum(src, seg, n)
kernel_name = 'mk_adaln_d1_jaxref_r8_bb1eda'

def setup_inputs(seed: int=0):
    np.random.seed(seed)
    _w = jnp.asarray

    def _L0_attn_setup():
        import jax, jax.numpy as jnp
        import numpy as np
        import math
        B, S, H = (1, 256, 512)
        NH, NKV, HD = (32, 8, 128)
        GS = 128
        WBITS = 4
        ZERO = float(2 ** (WBITS - 1))
        THETA = 10000.0

        def _dequant_matmul(x, qw, scales):
            w = (qw.astype(jnp.float32) - ZERO) * jnp.repeat(scales, GS, axis=0)
            return x @ w

        def _rope_tables(seq_len, dtype):
            inv_freq = 1.0 / THETA ** (jnp.arange(0, HD, 2, dtype=jnp.float32) / HD)
            freqs = jnp.arange(seq_len, dtype=jnp.float32)[:, None] * inv_freq
            emb = jnp.concatenate([freqs, freqs], axis=-1)
            return (jnp.cos(emb).astype(dtype), jnp.sin(emb).astype(dtype))

        def _rotate_half(x):
            x1, x2 = jnp.split(x, 2, axis=-1)
            return jnp.concatenate([-x2, x1], axis=-1)

        def _apply_rope(x, cos, sin):
            return x * cos[None, None] + _rotate_half(x) * sin[None, None]
        key = jax.random.key(seed)
        ks = jax.random.split(key, 9)
        small = lambda k, shp: jax.random.uniform(k, shp, jnp.float32) * 0.01 + 0.001
        return {'hidden_states': jax.random.normal(ks[0], (B, S, H), jnp.float32), 'scales_q': small(ks[1], (H // GS, NH * HD)), 'scales_k': small(ks[2], (H // GS, NKV * HD)), 'scales_v': small(ks[3], (H // GS, NKV * HD)), 'scales_o': small(ks[4], (NH * HD // GS, H)), 'qw_q': jax.random.randint(ks[5], (H, NH * HD), 0, 2 ** WBITS, jnp.int32), 'qw_k': jax.random.randint(ks[6], (H, NKV * HD), 0, 2 ** WBITS, jnp.int32), 'qw_v': jax.random.randint(ks[7], (H, NKV * HD), 0, 2 ** WBITS, jnp.int32), 'qw_o': jax.random.randint(ks[8], (NH * HD, H), 0, 2 ** WBITS, jnp.int32)}
    _L0_attn_in = _L0_attn_setup()

    def _L0_ffn_setup():
        import jax, jax.numpy as jnp
        import numpy as np
        R = 16
        NUM_EXPERTS = 8
        TOP_K = 2
        LORA_ALPHA = 32
        SCALING = LORA_ALPHA / R
        key = jax.random.key(seed)
        ks = jax.random.split(key, 6)
        d_in, d_out = (512, 512)
        x = jax.random.normal(ks[0], (4, 256, d_in), dtype=jnp.float32)
        W_base = jax.random.normal(ks[1], (d_out, d_in), dtype=jnp.float32) * 0.02
        b_base = jax.random.normal(ks[2], (d_out,), dtype=jnp.float32) * 0.02
        W_router = jax.random.normal(ks[3], (NUM_EXPERTS, d_in), dtype=jnp.float32) * 0.01
        A = jax.random.normal(ks[4], (NUM_EXPERTS, R, d_in), dtype=jnp.float32) * 0.02
        B = jax.random.normal(ks[5], (NUM_EXPERTS, d_out, R), dtype=jnp.float32) * 0.02
        return {'x': x, 'W_base': W_base, 'b_base': b_base, 'W_router': W_router, 'A': A, 'B': B}
    _L0_ffn_in = _L0_ffn_setup()
    _L0_c = _w((lambda *s: np.random.randn(*s).astype(np.float32) * 0.05)(1, 512))
    _L0_wmod = _w((lambda *s: np.random.randn(*s).astype(np.float32) * 0.05)(512, 6 * 512) * 512 ** (-0.5))
    _d = {'L0_attn_hidden_states': _L0_attn_in['hidden_states'], 'L0_attn_scales_q': _L0_attn_in['scales_q'], 'L0_attn_scales_k': _L0_attn_in['scales_k'], 'L0_attn_scales_v': _L0_attn_in['scales_v'], 'L0_attn_scales_o': _L0_attn_in['scales_o'], 'L0_attn_qw_q': _L0_attn_in['qw_q'], 'L0_attn_qw_k': _L0_attn_in['qw_k'], 'L0_attn_qw_v': _L0_attn_in['qw_v'], 'L0_attn_qw_o': _L0_attn_in['qw_o'], 'L0_ffn_W_base': _L0_ffn_in['W_base'], 'L0_ffn_b_base': _L0_ffn_in['b_base'], 'L0_ffn_W_router': _L0_ffn_in['W_router'], 'L0_ffn_A': _L0_ffn_in['A'], 'L0_ffn_B': _L0_ffn_in['B'], 'L0_c': _L0_c, 'L0_wmod': _L0_wmod}
    _x0 = _d['L0_attn_hidden_states']
    _d['L0_attn_hidden_states'] = jax.random.normal(jax.random.fold_in(jax.random.key(seed), 1), (1, 1024, 512), dtype=_x0.dtype)
    del _x0
    return _d

def reference(L0_attn_hidden_states, L0_attn_scales_q, L0_attn_scales_k, L0_attn_scales_v, L0_attn_scales_o, L0_attn_qw_q, L0_attn_qw_k, L0_attn_qw_v, L0_attn_qw_o, L0_ffn_W_base, L0_ffn_b_base, L0_ffn_W_router, L0_ffn_A, L0_ffn_B, L0_c, L0_wmod):

    def _L0_attn_ref(hidden_states, scales_q, scales_k, scales_v, scales_o, qw_q, qw_k, qw_v, qw_o):
        import jax, jax.numpy as jnp
        import numpy as np
        import math
        B, S, H = (1, 256, 512)
        NH, NKV, HD = (32, 8, 128)
        GS = 128
        WBITS = 4
        ZERO = float(2 ** (WBITS - 1))
        THETA = 10000.0

        def _dequant_matmul(x, qw, scales):
            w = (qw.astype(jnp.float32) - ZERO) * jnp.repeat(scales, GS, axis=0)
            return x @ w

        def _rope_tables(seq_len, dtype):
            inv_freq = 1.0 / THETA ** (jnp.arange(0, HD, 2, dtype=jnp.float32) / HD)
            freqs = jnp.arange(seq_len, dtype=jnp.float32)[:, None] * inv_freq
            emb = jnp.concatenate([freqs, freqs], axis=-1)
            return (jnp.cos(emb).astype(dtype), jnp.sin(emb).astype(dtype))

        def _rotate_half(x):
            x1, x2 = jnp.split(x, 2, axis=-1)
            return jnp.concatenate([-x2, x1], axis=-1)

        def _apply_rope(x, cos, sin):
            return x * cos[None, None] + _rotate_half(x) * sin[None, None]
        b, s, _ = hidden_states.shape
        q = _dequant_matmul(hidden_states, qw_q, scales_q).reshape(b, s, NH, HD).transpose(0, 2, 1, 3)
        k = _dequant_matmul(hidden_states, qw_k, scales_k).reshape(b, s, NKV, HD).transpose(0, 2, 1, 3)
        v = _dequant_matmul(hidden_states, qw_v, scales_v).reshape(b, s, NKV, HD).transpose(0, 2, 1, 3)
        cos, sin = _rope_tables(s, hidden_states.dtype)
        q = _apply_rope(q, cos, sin)
        k = _apply_rope(k, cos, sin)
        rep = NH // NKV
        k = jnp.repeat(k, rep, axis=1)
        v = jnp.repeat(v, rep, axis=1)
        scores = jnp.einsum('bhqd,bhkd->bhqk', q, k) / math.sqrt(HD)
        causal = jnp.tril(jnp.ones((s, s), dtype=bool))
        scores = jnp.where(causal[None, None], scores, jnp.finfo(scores.dtype).min)
        attn = jax.nn.softmax(scores.astype(jnp.float32), axis=-1).astype(q.dtype)
        ctx = jnp.einsum('bhqk,bhkd->bhqd', attn, v)
        ctx = ctx.transpose(0, 2, 1, 3).reshape(b, s, NH * HD)
        return _dequant_matmul(ctx, qw_o, scales_o)

    def _L0_ffn_ref(x, W_base, b_base, W_router, A, B):
        import jax, jax.numpy as jnp
        import numpy as np
        R = 16
        NUM_EXPERTS = 8
        TOP_K = 2
        LORA_ALPHA = 32
        SCALING = LORA_ALPHA / R
        orig_shape = x.shape
        d_in = x.shape[-1]
        x_flat = x.reshape(-1, d_in)
        logits = x_flat @ W_router.T
        probs = jax.nn.softmax(logits, axis=-1)
        topk_probs, topk_idx = jax.lax.top_k(probs, TOP_K)
        topk_probs = topk_probs / jnp.sum(topk_probs, axis=-1, keepdims=True)
        onehot = jax.nn.one_hot(topk_idx, NUM_EXPERTS, dtype=x.dtype)
        combine = jnp.einsum('nk,nke->ne', topk_probs, onehot)
        h = jnp.einsum('nd,erd->ner', x_flat, A)
        hw = h * combine[:, :, None]
        expert_out = jnp.einsum('ner,eor->no', hw, B) * SCALING
        base_out = x_flat @ W_base.T + b_base
        out = base_out + expert_out
        return out.reshape(*orig_shape[:-1], W_base.shape[0])
    x = L0_attn_hidden_states
    mod = (_silu(L0_c) @ L0_wmod).reshape(L0_c.shape[0], 6, 1, -1)
    sa, ca, ga, sb, cb, gb = (mod[:, 0], mod[:, 1], mod[:, 2], mod[:, 3], mod[:, 4], mod[:, 5])
    ga = (2 * (ga >= 0) - 1) * jnp.maximum(jnp.abs(ga), 0.25)
    gb = (2 * (gb >= 0) - 1) * jnp.maximum(jnp.abs(gb), 0.25)
    h = _layernorm(x, axis=-1) * (1 + ca) + sa
    x = x + ga * _L0_attn_ref(h, L0_attn_scales_q, L0_attn_scales_k, L0_attn_scales_v, L0_attn_scales_o, L0_attn_qw_q, L0_attn_qw_k, L0_attn_qw_v, L0_attn_qw_o)
    h = _layernorm(x, axis=-1) * (1 + cb) + sb
    x = x + gb * _L0_ffn_ref(h, L0_ffn_W_base, L0_ffn_b_base, L0_ffn_W_router, L0_ffn_A, L0_ffn_B)
    return x

_drawn_inputs = setup_inputs


def setup_inputs(seed=0):
    import zlib

    import numpy as np

    out = dict(_drawn_inputs(seed))
    spreads = {}
    factors = {'L0_attn_scales_q': 8.0,
     'L0_attn_scales_k': 8.0,
     'L0_attn_scales_v': 3.911,
     'L0_attn_scales_o': 4.145,
     'L0_ffn_b_base': 61.263,
     'L0_ffn_W_router': 5.125,
     'L0_ffn_A': 4.42,
     'L0_ffn_B': 4.434,
     'L0_ffn_W_base': 2.676}
    for name, (base, spread) in spreads.items():
        noise = np.random.default_rng([zlib.crc32(name.encode()), seed]).standard_normal(out[name].shape)
        drawn = base * np.exp(spread * noise) if base else spread * noise
        out[name] = jnp.asarray(drawn.astype(out[name].dtype))
    for name, factor in factors.items():
        out[name] = (out[name] * factor).astype(out[name].dtype)
    return out
```

```python
import math
from contextlib import ExitStack

import numpy as np

import concourse.bass as bass
import concourse.mybir as mybir
from concourse.alu_op_type import AluOpType as ALU

F32, F32R, BF16, I32 = mybir.dt.float32, mybir.dt.float32r, mybir.dt.bfloat16, mybir.dt.int32
ACT = mybir.ActivationFunctionType
AX = mybir.AxisListType

P = 128
S, H, HD = 1024, 512, 128
NKV, REP = 8, 4
KT = H // P
ST = S // P
CH = 512
GC = (REP + 2) * HD
E, R = 8, 16
ER = E * R
EPS, ZERO, SCALING = 1e-5, 8.0, 2.0
SCALE = 1.0 / math.sqrt(HD)

STEPS = ST
HEAD_UNITS = STEPS * REP
KEY_UNITS = STEPS * (STEPS + 1) // 2
PROJ = REP + 2
ROPES = 2 * (REP + 1)
VT = 2
WOUT, WQKV = REP, KT


def key_unit(t, kb):
    return t * (t + 1) // 2 + kb


def lap_order(last):
    out, values, closed = [], [], []

    def transposed(t, kb):
        out.append(("T", t, kb))
        values.append((t, kb))
        if len(values) > 2:
            times_values()

    def times_values():
        t, kb = values.pop(0)
        out.append(("V", t, kb))
        for c in list(closed):
            if (t, kb) != (c, c):
                out.append(("O", c))
                closed.remove(c)
        if kb == t:
            closed.append(t)

    for t in range(STEPS):
        n = t
        for h in range(REP):
            out.append(("S", t, h))
            for kb in range(h * n // REP, (h + 1) * n // REP):
                transposed(t - 1, kb)
    if not last:
        for j in range(PROJ):
            out.append(("P", j))
    for kb in range(STEPS):
        transposed(STEPS - 1, kb)
    while values:
        times_values()
    for c in closed:
        out.append(("O", c))
    if not last:
        out += [("X", c) for c in range(VT)]
    return out


def build(nc, hid, qkv_w, qkv_s, o_w, o_s, ffn_w, ffn_b, lora_b, c_in, wmod, cos_t, sin_t, ident_t,
          mask_t, spread_t, rank_t, out):
    ctx = ExitStack()
    with ctx:
        def sb(name, shape, dt):
            return ctx.enter_context(nc.sbuf_tensor(name, shape, dt))

        def sem(name):
            return ctx.enter_context(nc.semaphore(name))

        h_hi, h_lo = sb("h_hi", [P, KT, S], F32R), sb("h_lo", [P, KT, S], F32R)
        w_hi, w_lo = sb("w_hi", [P, KT, GC], F32R), sb("w_lo", [P, KT, GC], F32R)
        wo_hi, wo_lo = sb("wo_hi", [P, REP, H], F32R), sb("wo_lo", [P, REP, H], F32R)
        w_int = sb("w_int", [P, 2, GC], I32)
        w_f32 = sb("w_f32", [P, 2, GC], F32)
        q_hi, q_lo = sb("q_hi", [P, REP, S], F32R), sb("q_lo", [P, REP, S], F32R)
        k_hi, k_lo = sb("k_hi", [P, S], F32R), sb("k_lo", [P, S], F32R)
        v_hi, v_lo = sb("v_hi", [P, ST, HD], F32R), sb("v_lo", [P, ST, HD], F32R)
        prob_even = sb("prob_even", [P, REP * (STEPS - 1) * P], F32)
        prob_odd = sb("prob_odd", [P, REP * STEPS * P], F32)
        pt_hi, pt_lo = sb("pt_hi", [P, 2, CH], F32R), sb("pt_lo", [P, 2, CH], F32R)
        ctx_hi, ctx_lo = sb("ctx_hi", [P, 2, CH], F32R), sb("ctx_lo", [P, 2, CH], F32R)
        acc = sb("acc", [P, ST, H], F32)
        cos_s, sin_s = sb("cos_s", [P, S], F32), sb("sin_s", [P, S], F32)
        ident = sb("ident", [P, P], F32)
        ident16 = sb("ident16", [P, P], BF16)
        mask16 = sb("mask16", [P, P], BF16)
        neg_max = sb("neg_max", [P, HEAD_UNITS], F32)
        row_sum = sb("row_sum", [P, HEAD_UNITS], F32)
        inv_sum = sb("inv_sum", [P, HEAD_UNITS], F32)
        gates = sb("gates", [P, 2, H], F32)
        mod_col = sb("mod_col", [P, 4, KT], F32)
        small = sb("small", [P, 64], F32)
        parts = sb("parts", [P, ST, 6], F32)
        stats = sb("stats", [P, ST, 4], F32)

        bank = [ctx.enter_context(nc.psum_tensor(f"bank{i}", [P, 2 * CH if i < 2 else CH], F32))
                for i in range(6)]
        slots, pt_ps, ctx_ps, out_ps = bank[0:2], bank[2:4], bank[4], bank[5]

        rot_a = [prob_even[:, 512 + 1024 * i:1024 + 1024 * i] for i in range(2)]
        rot_b = [prob_even[:, 1024 + 1024 * i:1536 + 1024 * i] for i in range(2)]
        v_t = prob_even[:, 2560:3584]
        x_in = prob_odd[:, :].rearrange("p (t n) -> p t n", t=ST)
        h_f32 = [prob_even[:, CH * i:CH * i + CH] for i in range(2)]
        mod_w = acc[:, :, :].rearrange("p t n -> p (t n)").rearrange("p (k n) -> p k n", k=KT)
        mod_w2 = prob_odd[:, :].rearrange("p (k n) -> p k n", k=KT)

        lora_w, bias_row = prob_even[:, 1024:1536], prob_even[:, 1536:2048]
        rank, spread = prob_even[:, 2048:2112], prob_even[0:E, 2112:2240]
        r_exp, r_prob, r_tmp, *r_hot = (prob_even[:, 2240 + 64 * i:2304 + 64 * i].rearrange("p (t e) -> p t e", e=E)
                                        for i in range(5))
        logits_t = mix_t = prob_even[0:E, 2560:3584]
        mix_all, lora_f32 = prob_odd[:, 0:1024], prob_odd[:, 1024:2048]
        r_col = [small[:, 32 + ST * i:32 + ST * (i + 1)] for i in range(4)]

        def probs(t, h, a=0, b=None):
            width = (t + 1) * P
            b = width if b is None else b
            return (prob_odd if t % 2 else prob_even)[:, h * width + a:h * width + b]

        x_loaded = [sem(f"x_loaded{i}") for i in range(ST // 2)]
        c_loaded, mod_loaded, mod2_loaded = sem("c_loaded"), sem("mod_loaded"), sem("mod2_loaded")
        const_loaded, res_loaded, ffn_loaded = sem("const_loaded"), sem("res_loaded"), sem("ffn_loaded")
        w_loaded = [sem("w_loaded0"), sem("w_loaded1")]
        stored = sem("stored")
        ln_parts, ln_stats, ln_var, ln_rstd = sem("ln_parts"), sem("ln_stats"), sem("ln_var"), sem("ln_rstd")
        ln_normed, ln_turned = sem("ln_normed"), sem("ln_turned")
        h_affine, h_hi_done, h_lo_done = sem("h_affine"), sem("h_hi_done"), sem("h_lo_done")
        silu_exp, silu_done, silu_chain = sem("silu_exp"), sem("silu_done"), sem("silu_chain")
        mod_ps, mod_cols_done, mod_chain = sem("mod_ps"), sem("mod_cols_done"), sem("mod_chain")
        acc_zeroed, half_set = sem("acc_zeroed"), sem("half_set")
        slot_filled = sem("slot_filled")
        pt_filled = sem("pt_filled")
        pv_done = sem("pv_done")
        out_filled = sem("out_filled")
        w_scaled, w_hi_done, w_lo_done = sem("w_scaled"), sem("w_hi_done"), sem("w_lo_done")
        max_done, exp_done, inv_done, prob_done = sem("max_done"), sem("exp_done"), sem("inv_done"), sem("prob_done")
        pt_hi_done, pt_lo_done = sem("pt_hi_done"), sem("pt_lo_done")
        ctx_hi_done, ctx_lo_done = sem("ctx_hi_done"), sem("ctx_lo_done")
        acc_done = sem("acc_done")
        prob_begun = sem("prob_begun")
        rot_mul, rot_sum, rot_hi, rot_lo = sem("rot_mul"), sem("rot_sum"), sem("rot_hi"), sem("rot_lo")
        vt_copied = sem("vt_copied")
        res_chain, mixed = sem("res_chain"), sem("mixed")
        logits_t_ps, logits_t_done, logits_ps = sem("logits_t_ps"), sem("logits_t_done"), sem("logits_ps")
        router_chain, router_in, router_exp = sem("router_chain"), sem("router_in"), sem("router_exp")
        mix_done, mix_t_ps, mix_t_done = sem("mix_done"), sem("mix_t_ps"), sem("mix_t_done")
        spread_ps, spread_done, lora_ps = sem("spread_ps"), sem("spread_done"), sem("lora_ps")
        lora_mixed, lora_hi_done, lora_lo_done = sem("lora_mixed"), sem("lora_hi_done"), sem("lora_lo_done")
        b_hi_done, b_lo_done = sem("b_hi_done"), sem("b_lo_done")
        ffn_ps, ffn_chain, ffn_done = sem("ffn_ps"), sem("ffn_chain"), sem("ffn_done")

        def filled_s(lap, t, h):
            return (HEAD_UNITS + PROJ) * lap + PROJ + REP * t + h + 1

        def filled_p(n, j):
            return (HEAD_UNITS + PROJ) * n + j + 1

        def bank_t(lap, t, kb):
            return (KEY_UNITS + VT) * lap + VT + key_unit(t, kb) + 1

        def bank_x(n, c):
            return (KEY_UNITS + VT) * n + c + 1

        def unit(lap, t, h):
            return HEAD_UNITS * lap + REP * t + h + 1

        def keys(lap, t, kb):
            return KEY_UNITS * lap + key_unit(t, kb) + 1

        def step(lap, t):
            return STEPS * lap + t + 2

        def rope(n, i):
            return ROPES * n + i + 1

        def qkv_piece(n, kt):
            return (WQKV + WOUT) * n + kt + 1

        def out_piece(lap, h):
            return (WQKV + WOUT) * lap + WQKV + h + 1

        def qkv_arrived(n, kt):
            return 16 * (WQKV + WOUT) * n + 32 * (kt // 2 + 1)

        def out_arrived(lap, h):
            return 16 * (WQKV + WOUT) * lap + 16 * WQKV + 32 * (h // 2 + 1)

        def ffn_arrived(kt):
            return 16 * (WQKV + WOUT) * NKV + 16 * (kt // 2 + 1)

        def rows(i, n):
            return slice(n * i, n * (i + 1)) if isinstance(i, int) else bass.ds(i * n, n)

        def tile_of(j):
            return (k_hi[:, :], k_lo[:, :]) if j == 0 else (q_hi[:, j - 1, :], q_lo[:, j - 1, :])

        f32 = lambda ap: ap.bitcast(F32)
        ln_bank = [slots[i // 2][:, (i % 2) * CH:(i % 2 + 1) * CH] for i in range(4)]
        ln_src = [x_in, acc]

        block = ctx.enter_context(nc.Block())

        @block.sync
        def _(sp):
            def piece(i, slot, weights, scales, width):
                if i is not None:
                    sp.wait_ge(w_lo_done, i - 2)
                sp.dma_start(w_int[:, slot, 0:width], weights).then_inc(w_loaded[slot], 16)
                sp.dma_start(w_f32[:, slot, 0:width], scales.to_broadcast([P, width])).then_inc(w_loaded[slot], 16)

            def qkv_pieces(n, first=False):
                for kt in range(KT):
                    piece(None if first and kt < 2 else qkv_piece(n, kt), kt % 2,
                          qkv_w[rows(n * KT + kt, P), :], qkv_s[rows(n * KT + kt, 1), :], GC)

            def out_pieces(n):
                for h in range(REP):
                    piece(out_piece(n, h), h % 2, o_w[rows(n * REP + h, P), :], o_s[rows(n * REP + h, 1), :], H)

            sp.dma_start(small[:, 0:KT], c_in).then_inc(c_loaded, 16)
            for i in range(ST // 2):
                sp.dma_start(x_in[:, 2 * i:2 * i + 2, :],
                             hid[2 * i * P:2 * (i + 1) * P, :].rearrange("(t p) n -> p t n", p=P)).then_inc(x_loaded[i], 16)
            sp.dma_start(mod_w, wmod[:, 0:2 * H].rearrange("(k p) n -> p k n", p=P)).then_inc(mod_loaded, 16)
            sp.dma_start(ident[:, :], ident_t).then_inc(const_loaded, 16)
            sp.dma_start(cos_s[:, :], cos_t).then_inc(const_loaded, 16)
            sp.dma_start(sin_s[:, :], sin_t).then_inc(const_loaded, 16)
            sp.dma_start(prob_even[:, 0:P], mask_t).then_inc(const_loaded, 16)
            qkv_pieces(0, first=True)
            sp.wait_ge(mod_ps, 1)
            sp.dma_start(mod_w, wmod[:, 2 * H:4 * H].rearrange("(k p) n -> p k n", p=P)).then_inc(mod2_loaded, 16)
            sp.wait_ge(ln_turned, 2 * KT)
            sp.dma_start(mod_w2, wmod[:, 4 * H:6 * H].rearrange("(k p) n -> p k n", p=P)).then_inc(mod2_loaded, 16)
            with sp.Fori(0, NKV - 1) as lap:
                out_pieces(lap)
                qkv_pieces(lap + 1)
            out_pieces(NKV - 1)
            for kt in range(KT):
                sp.wait_ge(w_lo_done, qkv_piece(NKV, kt) - 2)
                sp.dma_start(w_f32[:, kt % 2, :], ffn_w[kt * P:(kt + 1) * P, :]).then_inc(w_loaded[kt % 2], 16)
            sp.wait_ge(pv_done, keys(NKV - 1, STEPS - 1, STEPS - 1))
            sp.dma_start(x_in, hid.rearrange("(t p) n -> p t n", p=P)).then_inc(res_loaded, 16)
            for dst, src in ((lora_w, lora_b), (bias_row, ffn_b.to_broadcast([P, H])), (rank, rank_t), (spread, spread_t)):
                sp.dma_start(dst, src).then_inc(ffn_loaded, 16)
            for t in range(ST):
                sp.wait_ge(ffn_done, t + 1)
                sp.dma_start(out[t * P:(t + 1) * P, :], acc[:, t, :]).then_inc(stored, 16)
            sp.wait_ge(stored, 16 * ST)

        @block.gpsimd
        def _(pool):
            def inverse_deviation(n):
                pool.wait_ge(ln_stats, ST * (n + 1))
                pool.tensor_scalar(stats[:, :, 2], stats[:, :, 1], EPS, 1.0, ALU.add, ALU.mult).then_inc(ln_var, 1)
                pool.wait_ge(ln_var, n + 1)
                pool.wait_ge(half_set, 1)
                pool.tensor_tensor(stats[:, :, 3], stats[:, :, 2], small[:, 24:24 + ST], ALU.pow).then_inc(ln_rstd, 1)

            def low_part(lo, full, hi, done):
                pool.tensor_tensor(lo, full, f32(hi), ALU.subtract).then_inc(done, 1)

            def rope_sum(n, j, c):
                i = 2 * j + c
                pool.wait_ge(rot_mul, rope(n, i))
                pool.tensor_tensor(rot_a[c], rot_a[c], rot_b[c], ALU.add).then_inc(rot_sum, 1)

            def rope_low(n, j, c):
                hi, lo = tile_of(j)
                pool.wait_ge(rot_hi, rope(n, 2 * j + c))
                low_part(lo[:, c * CH:(c + 1) * CH], rot_a[c], hi[:, c * CH:(c + 1) * CH], rot_lo)

            def projection(n, j):
                if j == PROJ - 1:
                    rope_low(n, REP, 1)
                    return
                for c in range(2):
                    rope_sum(n, j, c)
                    if (j, c) != (0, 0):
                        rope_low(n, *((j, 0) if c else (j - 1, 1)))

            def piece_low(hi, lo, slot, width, i):
                pool.wait_ge(w_hi_done, i)
                low_part(lo, w_f32[:, slot, 0:width], hi, w_lo_done)

            def qkv_low(n, kt):
                piece_low(w_hi[:, kt, :], w_lo[:, kt, :], kt % 2, GC, qkv_piece(n, kt))

            def lap_work(lap, last):
                for kind, a, *b in lap_order(last):
                    if kind == "S":
                        t, h = a, b[0]
                        pool.wait_ge(inv_done, unit(lap, t, h))
                        pool.sem_inc(prob_begun, 1)
                        pool.tensor_scalar(probs(t, h), probs(t, h), inv_sum[:, REP * t + h:REP * t + h + 1], 1.0,
                                           ALU.mult, ALU.mult).then_inc(prob_done, 1)
                        if t == 0:
                            piece_low(wo_hi[:, h, :], wo_lo[:, h, :], h % 2, H, out_piece(lap, h))
                        if t == 3:
                            qkv_low(lap + 1, h)
                    if kind == "P":
                        projection(lap + 1, a)

            pool.memset(small[:, 24:24 + ST], -0.5).then_inc(half_set, 1)
            inverse_deviation(0)
            for kt in range(KT):
                qkv_low(0, kt)
            for j in range(PROJ):
                projection(0, j)
            pool.wait_ge(mod_ps, 4)
            pool.memset(acc[:, :, :], 0.0).then_inc(acc_zeroed, 1)
            with pool.Fori(0, NKV - 1) as lap:
                lap_work(lap, False)
            lap_work(NKV - 1, True)
            pool.wait_ge(b_hi_done, 1)
            low_part(wo_lo[:, 0, :], lora_w, wo_hi[:, 0, :], b_lo_done)
            inverse_deviation(1)

        @block.scalar
        def _(act):
            def copy(dst, src, done):
                act.activation(dst, src, ACT.Copy).then_inc(done, 1)

            def affine(n):
                act.wait_ge(mod_cols_done, n + 1)
                for i in range(2 * KT):
                    kt, c = i // 2, i % 2
                    act.wait_ge(ln_turned, 2 * KT * n + i + 1)
                    if i >= 2:
                        act.wait_ge(h_lo_done, 2 * KT * n + i - 1)
                    act.activation(h_f32[i % 2], ln_bank[i % 4], ACT.Identity, bias=mod_col[:, 2 * n, kt:kt + 1],
                                   scale=mod_col[:, 2 * n + 1, kt:kt + 1]).then_inc(h_affine, 1)
                    act.wait_ge(h_affine, 2 * KT * n + i + 1)
                    copy(h_hi[:, kt, c * CH:(c + 1) * CH], h_f32[i % 2], h_hi_done)

            def qkv_high(n, kt):
                if not isinstance(n, int) or n > 0:
                    act.wait_ge(slot_filled, filled_p(n - 1, PROJ - 1))
                act.wait_ge(w_scaled, qkv_piece(n, kt))
                copy(w_hi[:, kt, :], w_f32[:, kt % 2, :], w_hi_done)

            def projection(n, j):
                if j < PROJ - 1:
                    hi, _lo = tile_of(j)
                    for c in range(2):
                        act.wait_ge(rot_sum, rope(n, 2 * j + c))
                        copy(hi[:, c * CH:(c + 1) * CH], rot_a[c], rot_hi)
                else:
                    act.wait_ge(slot_filled, filled_p(n, j))
                    copy(v_t, slots[j % 2][:, :], vt_copied)

            def values_high(n, c):
                act.wait_ge(pt_filled, bank_x(n, c))
                copy(v_hi[:, REP * c:REP * (c + 1), :], pt_ps[c][:, :].rearrange("p (t d) -> p t d", d=HD), pt_hi_done)

            def exponentials(lap, t, h):
                u = REP * t + h
                act.wait_ge(max_done, unit(lap, t, h))
                act.activation(probs(t, h), slots[u % 2][:, 0:(t + 1) * P], ACT.Exp, bias=neg_max[:, u:u + 1],
                               scale=1.0, accum_out=row_sum[:, u:u + 1]).then_inc(exp_done, 1)

            def lap_work(lap, last):
                waiting = []
                for kind, a, *b in lap_order(last):
                    if kind == "S":
                        while waiting:
                            exponentials(lap, *waiting.pop(0))
                        t, h = a, b[0]
                        waiting.append((t, h))
                        if t == 0:
                            act.wait_ge(out_filled, step(lap, 0) - 1)
                            act.wait_ge(w_scaled, out_piece(lap, h))
                            copy(wo_hi[:, h, :], w_f32[:, h % 2, 0:H], w_hi_done)
                        if t == 3 and not last:
                            qkv_high(lap + 1, h)
                        if t == 3 and last:
                            act.wait_ge(w_loaded[h % 2], ffn_arrived(h))
                            copy(w_hi[:, h, :], w_f32[:, h % 2, :], w_hi_done)
                    if kind == "T":
                        u = key_unit(a, b[0])
                        act.wait_ge(pt_filled, bank_t(lap, a, b[0]))
                        if u >= 2:
                            act.wait_ge(pv_done, keys(lap, a, b[0]) - 2)
                        copy(pt_hi[:, u % 2, :], pt_ps[u % 2][:, :], pt_hi_done)
                    while waiting and kind != "S":
                        exponentials(lap, *waiting.pop(0))
                    if kind == "V" and a == b[0]:
                        act.wait_ge(pv_done, keys(lap, a, a))
                        copy(ctx_hi[:, a % 2, :], ctx_ps[:, :], ctx_hi_done)
                    if kind == "P":
                        projection(lap + 1, a)
                    if kind == "X":
                        values_high(lap + 1, a)

            act.wait_ge(c_loaded, 16)
            act.activation(small[:, 4:8], small[:, 0:4], ACT.Exp, scale=-1.0).then_inc(silu_exp, 1)
            act.wait_ge(const_loaded, 64)
            act.activation(ident16[:, :], ident[:, :], ACT.Copy)
            copy(mask16[:, :], prob_even[:, 0:P], const_loaded)
            affine(0)
            for kt in range(KT):
                qkv_high(0, kt)
            for j in range(PROJ):
                projection(0, j)
            for c in range(VT):
                values_high(0, c)
            act.sem_inc(ctx_hi_done, 1)
            with act.Fori(0, NKV - 1) as lap:
                lap_work(lap, False)
            lap_work(NKV - 1, True)

            act.wait_ge(ffn_loaded, 64)
            act.wait_ge(out_filled, step(NKV - 1, STEPS - 1))
            copy(wo_hi[:, 0, :], lora_w, b_hi_done)
            affine(1)
            act.wait_ge(logits_t_ps, 1)
            copy(logits_t, slots[0][0:E, :], logits_t_done)
            act.wait_ge(router_in, 1)
            act.activation(r_exp, r_exp, ACT.Exp).then_inc(router_exp, 1)
            act.wait_ge(mix_t_ps, 1)
            copy(mix_t, slots[0][0:E, :], mix_t_done)
            act.wait_ge(spread_ps, 1)
            copy(mix_all, slots[1][:, :], spread_done)
            for c in range(2):
                act.wait_ge(lora_mixed, c + 1)
                copy(q_hi[:, 0, c * CH:(c + 1) * CH], lora_f32[:, c * CH:(c + 1) * CH], lora_hi_done)

        @block.vector
        def _(dve):
            def layernorm(n):
                src = ln_src[n]
                for t in range(ST):
                    dve.wait_ge(*((x_loaded[t // 2], 16) if n == 0 else (mixed, t + 1)))
                    dve.bn_stats(parts[:, t, :], src[:, t, :]).then_inc(ln_parts, 1)
                for t in range(ST):
                    dve.wait_ge(ln_parts, ST * n + t + 1)
                    dve.bn_aggr(stats[:, t, 0:2], parts[:, t, :]).then_inc(ln_stats, 1)
                dve.wait_ge(ln_stats, ST * (n + 1))
                dve.wait_ge(ln_rstd, n + 1)
                for t in range(ST):
                    dve.tensor_scalar(x_in[:, t, :], src[:, t, :], stats[:, t, 0:1], stats[:, t, 3:4],
                                      ALU.subtract, ALU.mult).then_inc(ln_normed, 1)

            def h_low(n):
                for i in range(2 * KT):
                    kt, c = i // 2, i % 2
                    dve.wait_ge(h_hi_done, 2 * KT * n + i + 1)
                    dve.tensor_tensor(h_lo[:, kt, c * CH:(c + 1) * CH], h_f32[i % 2],
                                      f32(h_hi[:, kt, c * CH:(c + 1) * CH]), ALU.subtract).then_inc(h_lo_done, 1)

            def scale_piece(slot, width, arrived):
                dve.wait_ge(w_loaded[slot], arrived)
                dve.scalar_tensor_tensor(w_f32[:, slot, 0:width], w_int[:, slot, 0:width], -ZERO,
                                         w_f32[:, slot, 0:width], ALU.add, ALU.mult).then_inc(w_scaled, 1)

            def projection(n, j):
                if j == PROJ - 1:
                    return
                scale = 1.0 if j == 0 else SCALE
                dve.wait_ge(slot_filled, filled_p(n, j))
                for c in range(2):
                    i, half, cols = 2 * j + c, HD // 2, slice(c * CH, (c + 1) * CH)
                    if i >= 2 or not isinstance(n, int) or n > 0:
                        dve.wait_ge(rot_lo, rope(n, i) - 2)
                    ps = slots[j % 2][:, cols]
                    dve.scalar_tensor_tensor(rot_a[c], ps, scale, cos_s[:, cols], ALU.mult, ALU.mult)
                    dve.scalar_tensor_tensor(rot_b[c][0:half], ps[half:HD], scale, sin_s[0:half, cols],
                                             ALU.mult, ALU.mult)
                    dve.scalar_tensor_tensor(rot_b[c][half:HD], ps[0:half], scale, sin_s[half:HD, cols],
                                             ALU.mult, ALU.mult).then_inc(rot_mul, 1)

            def values_low(n, c):
                dve.wait_ge(pt_hi_done, bank_x(n, c))
                cols = slice(REP * c, REP * (c + 1))
                dve.tensor_tensor(v_lo[:, cols, :], pt_ps[c][:, :].rearrange("p (t d) -> p t d", d=HD),
                                  f32(v_hi[:, cols, :]), ALU.subtract).then_inc(pt_lo_done, 1)

            def inverse(lap, t, h):
                u = REP * t + h
                dve.wait_ge(exp_done, unit(lap, t, h))
                dve.reciprocal(inv_sum[:, u:u + 1], row_sum[:, u:u + 1]).then_inc(inv_done, 1)

            def accumulate(lap, t):
                dve.wait_ge(out_filled, step(lap, t))
                dve.tensor_tensor(acc[:, t, :], out_ps[:, :], acc[:, t, :], ALU.add).then_inc(acc_done, 1)

            def lap_work(lap, last):
                sums, outs = [], []
                for kind, a, *b in lap_order(last):
                    if kind == "S":
                        t, h = a, b[0]
                        u = REP * t + h
                        dve.wait_ge(slot_filled, filled_s(lap, t, h))
                        dve.tensor_reduce(neg_max[:, u:u + 1], slots[u % 2][:, 0:(t + 1) * P], AX.X, ALU.max,
                                          negate=True).then_inc(max_done, 1)
                        if t == 0:
                            scale_piece(h % 2, H, out_arrived(lap, h))
                        if t == 3 and not last:
                            scale_piece(h % 2, GC, qkv_arrived(lap + 1, h))
                    if sums and (kind == "S" or kind == "P" or (kind == "T" and b[0] == 0)):
                        inverse(lap, *sums.pop(0))
                    if kind == "S":
                        sums.append((t, h))
                    if kind == "T":
                        u = key_unit(a, b[0])
                        dve.wait_ge(pt_hi_done, bank_t(lap, a, b[0]))
                        dve.tensor_tensor(pt_lo[:, u % 2, :], pt_ps[u % 2][:, :], f32(pt_hi[:, u % 2, :]),
                                          ALU.subtract).then_inc(pt_lo_done, 1)
                    if kind == "V" and a == b[0]:
                        dve.wait_ge(ctx_hi_done, step(lap, a))
                        dve.tensor_tensor(ctx_lo[:, a % 2, :], ctx_ps[:, :], f32(ctx_hi[:, a % 2, :]),
                                          ALU.subtract).then_inc(ctx_lo_done, 1)
                    outs = [(t, n - 1) for t, n in outs]
                    if outs and outs[0][1] <= 0:
                        accumulate(lap, outs.pop(0)[0])
                    if kind == "O":
                        outs.append((a, 4))
                    if kind == "P":
                        projection(lap + 1, a)
                    if kind == "X":
                        values_low(lap + 1, a)
                for t, _n in outs:
                    accumulate(lap, t)

            chained = [0]

            def link(chain, ins):
                chained[0] += 1
                ins.then_inc(chain, 1)
                dve.wait_ge(chain, chained[0])

            dve.wait_ge(silu_exp, 1)
            link(silu_chain, dve.tensor_scalar(small[:, 8:12], small[:, 4:8], 1.0, None, ALU.add))
            link(silu_chain, dve.reciprocal(small[:, 12:16], small[:, 8:12]))
            dve.tensor_tensor(small[:, 16:20], small[:, 0:4], small[:, 12:16], ALU.mult).then_inc(silu_done, 1)
            layernorm(0)
            dve.wait_ge(mod_ps, 1)
            dve.tensor_copy(mod_col[:, 0, :], ctx_ps[:, 0:KT])
            dve.tensor_scalar(mod_col[:, 1, :], ctx_ps[:, KT:2 * KT], 1.0, None, ALU.add).then_inc(mod_cols_done, 1)
            for kt in range(KT):
                scale_piece(kt % 2, GC, qkv_arrived(0, kt)) if kt < 2 else None
            h_low(0)
            for kt in range(2, KT):
                scale_piece(kt % 2, GC, qkv_arrived(0, kt))
            dve.wait_ge(const_loaded, 65)
            for j in range(PROJ):
                projection(0, j)
            for c in range(VT):
                values_low(0, c)
            dve.wait_ge(mod_ps, 2)
            dve.tensor_copy(mod_col[:, 2, :], out_ps[:, 0:KT])
            dve.tensor_scalar(mod_col[:, 3, :], out_ps[:, KT:2 * KT], 1.0, None, ALU.add).then_inc(mod_cols_done, 1)
            chained[0] = 0
            for i, ps in enumerate((ctx_ps, out_ps)):
                dve.wait_ge(mod_ps, 3 + i)
                gate, size = gates[:, i, :], prob_even[:, 0:H]
                link(mod_chain, dve.tensor_scalar(gate, ps[:, :], 0.0, 2.0, ALU.is_ge, ALU.mult))
                link(mod_chain, dve.tensor_scalar(gate, gate, -1.0, None, ALU.add))
                link(mod_chain, dve.tensor_tensor(size, ps[:, :], gate, ALU.mult))
                link(mod_chain, dve.scalar_tensor_tensor(gate, size, 0.25, gate, ALU.max, ALU.mult))
            dve.wait_ge(acc_zeroed, 1)
            dve.sem_inc(acc_done, 1)
            dve.sem_inc(ctx_lo_done, 1)
            with dve.Fori(0, NKV - 1) as lap:
                lap_work(lap, False)
            lap_work(NKV - 1, True)

            dve.wait_ge(res_loaded, 16)
            dve.wait_ge(acc_done, step(NKV - 1, STEPS - 1))
            for t in range(ST):
                dve.tensor_tensor(acc[:, t, :], acc[:, t, :], gates[:, 0, :], ALU.mult).then_inc(res_chain, 1)
            for t in range(ST):
                dve.wait_ge(res_chain, t + 1)
                dve.tensor_tensor(acc[:, t, :], acc[:, t, :], x_in[:, t, :], ALU.add).then_inc(mixed, 1)
            layernorm(1)
            h_low(1)

            dve.wait_ge(logits_ps, 1)
            chained[0] = 0
            wide = [P, ST, E]

            def all_experts(col):
                return col.unsqueeze(2).to_broadcast(wide)

            def routed(ins):
                link(router_chain, ins)

            logits = slots[1][:, 0:ST * E].rearrange("p (t e) -> p t e", e=E)
            routed(dve.tensor_reduce(r_col[0], logits, AX.X, ALU.max))
            dve.tensor_tensor(r_exp, logits, all_experts(r_col[0]), ALU.subtract).then_inc(router_in, 1)
            dve.wait_ge(router_exp, 1)
            routed(dve.tensor_reduce(r_col[0], r_exp, AX.X, ALU.add))
            routed(dve.reciprocal(r_col[1], r_col[0]))
            routed(dve.tensor_tensor(r_prob, r_exp, all_experts(r_col[1]), ALU.mult))
            for i in range(2):
                src, top = (r_prob, r_exp)[i], r_col[2 + i]
                routed(dve.tensor_reduce(top, src, AX.X, ALU.max))
                routed(dve.tensor_tensor(r_tmp, src, all_experts(top), ALU.is_equal))
                routed(dve.tensor_tensor(r_tmp, r_tmp, rank.rearrange("p (t e) -> p t e", e=E), ALU.mult))
                routed(dve.tensor_reduce(r_col[0], r_tmp, AX.X, ALU.max))
                routed(dve.tensor_tensor(r_hot[i], r_tmp, all_experts(r_col[0]), ALU.is_equal))
                if i == 0:
                    routed(dve.scalar_tensor_tensor(r_exp, r_hot[0], -2.0, r_prob, ALU.mult, ALU.add))
            routed(dve.tensor_tensor(r_col[0], r_col[2], r_col[3], ALU.add))
            routed(dve.reciprocal(r_col[1], r_col[0]))
            for i in range(2):
                routed(dve.tensor_tensor(r_col[2 + i], r_col[2 + i], r_col[1], ALU.mult))
                routed(dve.tensor_tensor(r_hot[i], r_hot[i], all_experts(r_col[2 + i]), ALU.mult))
            dve.tensor_tensor(r_prob, r_hot[0], r_hot[1], ALU.add).then_inc(mix_done, 1)

            dve.wait_ge(spread_done, 1)
            dve.wait_ge(lora_ps, 1)
            for c in range(2):
                cols = slice(c * CH, (c + 1) * CH)
                dve.scalar_tensor_tensor(lora_f32[:, cols], pt_ps[c][:, :], SCALING, mix_all[:, cols],
                                         ALU.mult, ALU.mult).then_inc(lora_mixed, 1)
            for c in range(2):
                cols = slice(c * CH, (c + 1) * CH)
                dve.wait_ge(lora_hi_done, c + 1)
                dve.tensor_tensor(q_lo[:, 0, cols], lora_f32[:, cols], f32(q_hi[:, 0, cols]),
                                  ALU.subtract).then_inc(lora_lo_done, 1)
            for t in range(ST):
                ps = (ctx_ps, out_ps)[t % 2]
                dve.wait_ge(ffn_ps, t + 1)
                dve.tensor_tensor(x_in[:, 4 + t % 2, :], ps[:, :], bias_row, ALU.add).then_inc(ffn_chain, 1)
                dve.wait_ge(ffn_chain, 2 * t + 1)
                dve.tensor_tensor(x_in[:, 4 + t % 2, :], x_in[:, 4 + t % 2, :], gates[:, 1, :], ALU.mult).then_inc(ffn_chain, 1)
                dve.wait_ge(ffn_chain, 2 * t + 2)
                dve.tensor_tensor(acc[:, t, :], acc[:, t, :], x_in[:, 4 + t % 2, :], ALU.add).then_inc(ffn_done, 1)

        @block.tensor
        def _(pe):
            def product(dst, left, right, start, stop):
                pe.matmul(dst, left[0], right[0], start=start, stop=False)
                pe.matmul(dst, left[0], right[1], start=False, stop=False)
                return pe.matmul(dst, left[1], right[0], start=False, stop=stop)

            def turned(n):
                for i in range(2 * KT):
                    kt, c = i // 2, i % 2
                    if i >= 4:
                        pe.wait_ge(h_affine, 2 * KT * n + i - 3)
                    for r in range(4):
                        t = 4 * c + r
                        if kt == 0:
                            pe.wait_ge(ln_normed, ST * n + t + 1)
                        mm = pe.transpose(ln_bank[i % 4][:, r * P:(r + 1) * P], x_in[:, t, kt * P:(kt + 1) * P],
                                          ident[:, :])
                    mm.then_inc(ln_turned, 1)

            silu = small[:, 16:20]

            def mod_columns(dst, weights):
                for nt in range(KT):
                    for kt in range(KT):
                        mm = pe.matmul(dst[:, nt:nt + 1], weights[:, kt, nt * P:(nt + 1) * P], silu[:, kt:kt + 1],
                                       start=kt == 0, stop=kt == KT - 1)
                return mm

            def mod_rows(dst, weights):
                for kt in range(KT):
                    mm = pe.matmul(dst, silu[:, kt:kt + 1].to_broadcast([P, P]), weights[:, kt, :],
                                   start=kt == 0, stop=kt == KT - 1)
                return mm

            def projection(n, j):
                first = isinstance(n, int) and n == 0
                if j == 0:
                    if first:
                        pe.wait_ge(h_lo_done, 2 * KT)
                    else:
                        pe.wait_ge(exp_done, unit(n - 1, STEPS - 1, REP - 2))
                elif j == 1 and not first:
                    pe.wait_ge(exp_done, unit(n - 1, STEPS - 1, REP - 1))
                elif j >= 2:
                    pe.wait_ge(rot_mul, rope(n, 2 * (j - 2) + 1))
                cols = slice(j * HD, (j + 1) * HD)
                for kt in range(KT):
                    if j == 0:
                        pe.wait_ge(w_lo_done, qkv_piece(n, kt))
                    a, z = kt == 0, kt == KT - 1
                    for w, h, s, e in ((w_hi, h_hi, a, False), (w_hi, h_lo, False, False), (w_lo, h_hi, False, z)):
                        for c in range(2):
                            mm = pe.matmul(slots[j % 2][:, c * CH:(c + 1) * CH], w[:, kt, cols],
                                           h[:, kt, c * CH:(c + 1) * CH], start=s, stop=e)
                mm.then_inc(slot_filled, 1)

            def values_turned(n, c):
                first = isinstance(n, int) and n == 0
                pe.wait_ge(vt_copied, n + 1)
                if not first:
                    pe.wait_ge(pt_lo_done, bank_x(n, c) - 2)
                for r in range(4):
                    mm = pe.transpose(pt_ps[c][:, r * P:(r + 1) * P], v_t[:, (4 * c + r) * P:(4 * c + r + 1) * P],
                                      ident[:, :])
                mm.then_inc(pt_filled, 1)

            def scores(lap, t, h):
                u = REP * t + h
                if t == 0:
                    pe.wait_ge(rot_lo, rope(lap, 2 * (h + 1) + 1))
                if u == 0:
                    pe.wait_ge(rot_mul, rope(lap, ROPES - 1))
                elif u == 1:
                    pe.wait_ge(vt_copied, lap + 1)
                else:
                    pe.wait_ge(exp_done, unit(lap, t, h) - 2)
                rows_ = slice(t * P, (t + 1) * P)
                width = (t + 1) * P
                for c in range(0, width, CH):
                    e = min(width, c + CH)
                    dst = slots[u % 2][:, c:e]
                    qh, ql, kh, kl = q_hi[:, h, rows_], q_lo[:, h, rows_], k_hi[:, c:e], k_lo[:, c:e]
                    pe.matmul(dst, qh, kh, start=True, stop=False)
                    pe.matmul(dst, qh, kl, start=False, stop=False)
                    if e == width:
                        pe.matmul(slots[u % 2][:, width - P:width], ident16[:, :], mask16[:, :], start=False, stop=False)
                    mm = pe.matmul(dst, ql, kh, start=False, stop=True)
                mm.then_inc(slot_filled, 1)

            def lap_work(lap, last):
                for kind, a, *b in lap_order(last):
                    if kind == "S":
                        scores(lap, a, b[0])
                    if kind == "T":
                        t, kb = a, b[0]
                        u = key_unit(t, kb)
                        if kb == 0:
                            pe.wait_ge(prob_done, unit(lap, t, REP - 1))
                        pe.wait_ge(pt_lo_done, bank_t(lap, t, kb) - 2)
                        for h in range(REP):
                            mm = pe.transpose(pt_ps[u % 2][:, h * P:(h + 1) * P], probs(t, h, kb * P, (kb + 1) * P),
                                              ident[:, :])
                        mm.then_inc(pt_filled, 1)
                    if kind == "V":
                        t, kb = a, b[0]
                        u = key_unit(t, kb)
                        if kb == 0:
                            pe.wait_ge(ctx_lo_done, step(lap, t) - 1)
                        pe.wait_ge(pt_lo_done, bank_t(lap, t, kb))
                        product(ctx_ps[:, :], (v_hi[:, kb, :], v_lo[:, kb, :]), (pt_hi[:, u % 2, :], pt_lo[:, u % 2, :]),
                                kb == 0, kb == t).then_inc(pv_done, 1)
                    if kind == "O":
                        pe.wait_ge(ctx_lo_done, step(lap, a))
                        pe.wait_ge(acc_done, step(lap, a) - 1)
                        for h in range(REP):
                            if a == 0:
                                pe.wait_ge(w_lo_done, out_piece(lap, h))
                            cols = slice(h * P, (h + 1) * P)
                            mm = product(out_ps[:, :], (ctx_hi[:, a % 2, cols], ctx_lo[:, a % 2, cols]),
                                         (wo_hi[:, h, :], wo_lo[:, h, :]), h == 0, h == REP - 1)
                        mm.then_inc(out_filled, 1)
                    if kind == "P":
                        projection(lap + 1, a)
                    if kind == "X":
                        values_turned(lap + 1, a)

            pe.wait_ge(mod_loaded, 16)
            pe.wait_ge(silu_done, 1)
            mod_columns(ctx_ps[:, 0:KT], mod_w[:, :, 0:H])
            mod_columns(ctx_ps[:, KT:2 * KT], mod_w[:, :, H:2 * H]).then_inc(mod_ps, 1)
            pe.wait_ge(const_loaded, 65)
            turned(0)
            for j in range(PROJ):
                projection(0, j)
            for c in range(VT):
                values_turned(0, c)
            pe.wait_ge(mod2_loaded, 32)
            mod_columns(out_ps[:, 0:KT], mod_w[:, :, H:2 * H])
            mod_columns(out_ps[:, KT:2 * KT], mod_w2[:, :, 0:H]).then_inc(mod_ps, 1)
            pe.wait_ge(mod_cols_done, 1)
            mod_rows(ctx_ps[:, :], mod_w[:, :, 0:H]).then_inc(mod_ps, 1)
            pe.wait_ge(mod_cols_done, 2)
            mod_rows(out_ps[:, :], mod_w2[:, :, H:2 * H]).then_inc(mod_ps, 1)
            pe.sem_inc(out_filled, 1)
            pe.wait_ge(mod_chain, 7)
            with pe.Fori(0, NKV - 1) as lap:
                lap_work(lap, False)
            lap_work(NKV - 1, True)

            turned(1)
            pe.wait_ge(h_lo_done, 4 * KT)
            pe.wait_ge(h_affine, 4 * KT)
            pe.wait_ge(w_lo_done, qkv_piece(NKV, KT - 1))
            a_rows, r_rows = slice(H, H + ER), slice(H + ER, GC)
            for rows_, dst in ((r_rows, slots[0]), (a_rows, None)):
                for c in range(2):
                    bank_ = dst[:, c * CH:(c + 1) * CH] if dst is not None else pt_ps[c][:, :]
                    for kt in range(KT):
                        mm = product(bank_, (w_hi[:, kt, rows_], w_lo[:, kt, rows_]),
                                     (h_hi[:, kt, c * CH:(c + 1) * CH], h_lo[:, kt, c * CH:(c + 1) * CH]),
                                     kt == 0, kt == KT - 1)
                mm.then_inc(logits_t_ps if dst is not None else lora_ps, 1)
            pe.wait_ge(logits_t_done, 1)
            for t in range(ST):
                mm = pe.transpose(slots[1][:, t * E:(t + 1) * E], logits_t[:, t * P:(t + 1) * P], ident[0:E, 0:E])
            mm.then_inc(logits_ps, 1)

            def dense(t):
                pe.wait_ge(*((ffn_done, t - 1) if t >= 2 else (acc_done, step(NKV - 1, STEPS - 1))))
                for kt in range(KT):
                    product((ctx_ps, out_ps)[t % 2][:, :], (h_hi[:, kt, t * P:(t + 1) * P], h_lo[:, kt, t * P:(t + 1) * P]),
                            (w_hi[:, kt, 0:H], w_lo[:, kt, 0:H]), kt == 0, False)

            def experts(t):
                cols = slice(t * P, (t + 1) * P)
                product((ctx_ps, out_ps)[t % 2][:, :], (q_hi[:, 0, cols], q_lo[:, 0, cols]),
                        (wo_hi[:, 0, :], wo_lo[:, 0, :]), False, True).then_inc(ffn_ps, 1)

            dense(0)
            dense(1)
            pe.wait_ge(mix_done, 1)
            for t in range(ST):
                mm = pe.transpose(slots[0][0:E, t * P:(t + 1) * P], r_prob[:, t, :], ident[:, :])
            mm.then_inc(mix_t_ps, 1)
            pe.wait_ge(mix_t_done, 1)
            for c in range(2):
                mm = pe.matmul(slots[1][:, c * CH:(c + 1) * CH], spread, mix_t[:, c * CH:(c + 1) * CH], start=True, stop=True)
            mm.then_inc(spread_ps, 1)
            pe.wait_ge(lora_lo_done, 2)
            pe.wait_ge(b_lo_done, 1)
            for t in range(ST):
                if t >= 2:
                    dense(t)
                experts(t)


def rope_tables():
    inv = (1.0 / np.float32(10000.0) ** (np.arange(0, HD, 2, dtype=np.float32) / np.float32(HD))).astype(np.float32)
    freqs = np.arange(S, dtype=np.float32)[:, None] * inv
    emb = np.concatenate([freqs, freqs], axis=-1).T
    sign = np.where(np.arange(HD) < HD // 2, -1.0, 1.0).astype(np.float32)[:, None]
    return np.cos(emb).astype(np.float32), (np.sin(emb) * sign).astype(np.float32)


def kernel(**inputs):
    import concourse.bacc as bacc
    from concourse.bass_utils import run_bass_kernel_spmd

    x = {n.removeprefix("L0_"): np.asarray(a) for n, a in inputs.items()}

    def by_group(k, q, v):
        rows = k.shape[0]
        parts = [a.reshape(rows, NKV, -1) for a in (k, q, v)]
        return np.ascontiguousarray(np.concatenate(parts, axis=2).transpose(1, 0, 2)).reshape(NKV * rows, GC)

    cos_t, sin_t = rope_tables()
    tri = np.where(np.arange(P)[None, :] > np.arange(P)[:, None], np.float32(-1e30), np.float32(0))
    arrays = {
        "hid": x["attn_hidden_states"].reshape(S, H),
        "qkv_w": by_group(x["attn_qw_k"], x["attn_qw_q"], x["attn_qw_v"]),
        "qkv_s": by_group(x["attn_scales_k"], x["attn_scales_q"], x["attn_scales_v"]),
        "o_w": x["attn_qw_o"],
        "o_s": x["attn_scales_o"],
        "ffn_w": np.concatenate([x["ffn_W_base"].T, x["ffn_A"].reshape(ER, H).T, x["ffn_W_router"].T,
                                 np.zeros((H, GC - H - ER - E), np.float32)], axis=1),
        "ffn_b": x["ffn_b_base"].reshape(1, H),
        "lora_b": x["ffn_B"].transpose(0, 2, 1).reshape(ER, H),
        "c_in": x["c"].reshape(KT, P).T,
        "wmod": x["wmod"],
        "cos_t": cos_t,
        "sin_t": sin_t,
        "ident_t": np.eye(P, dtype=np.float32),
        "mask_t": tri.astype(np.float32),
        "spread_t": np.repeat(np.eye(E, dtype=np.float32), R, axis=1),
        "rank_t": np.tile(np.arange(E, 0, -1, dtype=np.float32), (P, ST)),
    }
    nc = bacc.Bacc("TRN2", target_bir_lowering=False, num_devices=1, dynamic_dma_scratch_size=1024)
    feed, args = {}, []
    for name, a in arrays.items():
        a = np.ascontiguousarray(a)
        feed[f"in_{name}"] = a
        args.append(nc.dram_tensor(f"in_{name}", a.shape, mybir.dt.from_np(a.dtype), kind="ExternalInput").ap())
    args.append(nc.dram_tensor("out_x", (S, H), F32, kind="ExternalOutput").ap())
    build(nc, *args)
    r = run_bass_kernel_spmd(nc, [feed], core_ids=[0])
    return r.results[0]["out_x"].reshape(1, S, H)
```

```python
import math
from contextlib import ExitStack

import numpy as np

import concourse.bass as bass
import concourse.mybir as mybir
from concourse.alu_op_type import AluOpType as ALU

F32, F32R, BF16, I32 = mybir.dt.float32, mybir.dt.float32r, mybir.dt.bfloat16, mybir.dt.int32
ACT = mybir.ActivationFunctionType
AX = mybir.AxisListType

P = 128
S, H, HD = 1024, 512, 128
NKV, REP = 8, 4
KT = H // P
ST = S // P
CH = 512
GC = (REP + 2) * HD
E, R = 8, 16
ER = E * R
EPS, ZERO, SCALING = 1e-5, 8.0, 2.0
SCALE = 1.0 / math.sqrt(HD)

STEPS = ST
HEAD_UNITS = STEPS * REP
KEY_UNITS = STEPS * (STEPS + 1) // 2
PROJ = REP + 2
ROPES = 2 * (REP + 1)
VT = 2
WOUT, WQKV = REP, KT


ORDER = (7, 0, 6, 1, 5, 2, 4, 3)
POS = {t: i for i, t in enumerate(ORDER)}
SLOTS = [("project", j, 0) for j in range(PROJ)] + [("scores", t, h) for t in ORDER for h in range(REP)]
KEYS = [(t, kb) for t in ORDER for kb in range(t + 1)]


def group_tasks():
    work = {}

    def add(engine, cost, kind, a=0, b=0, after=()):
        work[kind, a, b] = (engine, cost, list(after))

    def slot_reader(i):
        kind, a, b = SLOTS[i - 2]
        back = 0 if i >= 2 else 1
        if kind == "scores":
            return "exp", a, b, back
        return ("rotate", a, 1, back) if a < PROJ - 1 else ("v_copy", 0, 0, back)

    for j in range(PROJ):
        add("pe", 5.2, "project", j, 0, [slot_reader(j), ("low_qkv", KT - 1, 0, 0)])
    for i in range(ROPES):
        j, c = i // 2, i % 2
        room = [("turn", 2, 2, 1)] if i == 0 else []
        if i > 2:
            room.append(("rot_low", (i - 3) // 2, (i - 3) % 2, 0))
        if i > 1:
            room.append(("rot_sum", (i - 2) // 2, i % 2, 0))
        add("dve", 1.85, "rotate", j, c, [("project", j, 0, 0)] + room)
        add("pool", 1.3, "rot_sum", j, c, [("rotate", j, c, 0)])
        add("act", 0.55, "rot_high", j, c, [("rot_sum", j, c, 0)])
        add("pool", 1.3, "rot_low", j, c, [("rot_high", j, c, 0)])
    add("act", 1.1, "v_copy", 0, 0, [("project", PROJ - 1, 0, 0)])
    for c in range(VT):
        add("pe", 0.43, "turn_v", c, 0, [("v_copy", 0, 0, 0), ("values", ORDER[-1], ORDER[-1], 1)])
        add("act", 0.55, "v_high", c, 0, [("turn_v", c, 0, 0)])
        add("dve", 0.62, "v_low", c, 0, [("v_high", c, 0, 0)])
    for i, (kind, t, h) in enumerate(SLOTS):
        if kind == "scores":
            n, p = (t + 1) * P, POS[t]
            columns = sum(max(min(CH, n - c), 256) for c in range(0, n, CH))
            room = ("turn", ORDER[p - 4], ORDER[p - 4], 0 if p >= 4 else 1)
            add("pe", 3 * columns / 2400 + 0.06, kind, t, h, [slot_reader(i), ("rot_low", h + 1, 1, 0), room])
            add("dve", 0.14 + 1.04e-3 * n, "max", t, h, [("scores", t, h, 0)])
            add("act", 0.3 + 0.83e-3 * n, "exp", t, h, [("max", t, h, 0)])
            add("dve", 0.08, "inverse", t, h, [("exp", t, h, 0)])
            add("pool", 0.12 + 1.15e-3 * n, "norm", t, h, [("inverse", t, h, 0)])
    for i, (t, kb) in enumerate(KEYS):
        first, last, back = kb == 0, ORDER[POS[t] - 1], 0 if POS[t] else 1
        bank = ("low", *KEYS[i - 2], 0) if i >= 2 else ("v_low", i, 0, 0)
        add("pe", 0.43, "turn", t, kb, [bank, ("norm", t, REP - 1, 0)])
        add("act", 0.55, "high", t, kb, [("turn", t, kb, 0)] + [("values", *KEYS[i - 2], 0)] * (i >= 2))
        add("dve", 0.62, "low", t, kb, [("high", t, kb, 0)])
        add("pe", 0.65, "values", t, kb, [("low", t, kb, 0), ("v_low", 1, 0, 0)] + [("ctx_low", last, 0, back)] * first)
        if kb == t:
            add("act", 0.55, "ctx_high", t, 0, [("values", t, t, 0)])
            add("dve", 0.62, "ctx_low", t, 0, [("ctx_high", t, 0, 0)])
            add("pe", 2.6, "output", t, 0, [("ctx_low", t, 0, 0), ("low_o", REP - 1, 0, 0), ("add", last, 0, back)])
            add("dve", 0.62, "add", t, 0, [("output", t, 0, 0)])
    for i in range(4):
        add("dve", 0.62, "scale_o", i, 0, [("turn_v", 1, 0, 0)] + [("low_o", i - 2, 0, 0)] * (i >= 2))
        add("act", 0.55, "high_o", i, 0, [("scale_o", i, 0, 0), ("output", ORDER[-1], 0, 1)])
        add("pool", 1.3, "low_o", i, 0, [("high_o", i, 0, 0)])
        add("dve", 0.9, "scale_qkv", i, 0, [("low_o", i + 2, 0, 1) if i < 2 else ("low_qkv", i - 2, 0, 0)])
        add("act", 0.75, "high_qkv", i, 0, [("scale_qkv", i, 0, 0), ("project", PROJ - 1, 0, 1)])
        add("pool", 1.9, "low_qkv", i, 0, [("high_qkv", i, 0, 0)])
    return work


EARLY = ("project", "rotate", "rot_sum", "rot_high", "rot_low", "v_copy", "turn_v", "v_high", "v_low",
         "scale_qkv", "high_qkv", "low_qkv")
TOGETHER = {"project": "scores", "turn_v": "turn", "v_high": "high", "v_low": "low", "scale_qkv": "scale_o",
            "high_qkv": "high_o", "low_qkv": "low_o"}
SIGNAL, LOAD = 0.1, 5.0


def lap_orders(lead=9.0, laps=3):
    work = group_tasks()

    def early(task):
        return task[0] in EARLY or (task[0] in ("scores", "max", "exp", "inverse", "norm") and task[1] == ORDER[0])

    def rank(task):
        kind, a, b = task
        by_step = kind not in EARLY and kind not in ("scale_o", "high_o", "low_o")
        return kind not in EARLY, POS[a] if by_step else a, b

    sequences = {}
    for task in work:
        sequences.setdefault(TOGETHER.get(task[0], task[0]), []).append(task)
    after = {}
    for g in range(laps + 1):
        for task, (_engine, _cost, names) in work.items():
            after[g, task] = {(g - back, (k, a, b)) for k, a, b, back in names if g >= back}
        for sequence in sequences.values():
            sequence.sort(key=rank)
            for i, task in enumerate(sequence):
                if i or g:
                    after[g, task].add((g if i else g - 1, sequence[i - 1]))

    def lap_of(item):
        return item[0] - 1 if early(item[1]) else item[0]

    items = [x for x in after if lap_of(x) < laps]
    followers, open_ = {x: [] for x in items}, {}
    for x in items:
        open_[x] = len(after[x])
        for y in after[x]:
            followers[y].append(x)
    sorted_, count = [x for x in items if not open_[x]], dict(open_)
    for x in sorted_:
        for y in followers[x]:
            count[y] -= 1
            if not count[y]:
                sorted_.append(y)
    way = {}
    for x in reversed(sorted_):
        way[x] = work[x[1]][1] + SIGNAL + max((way[y] for y in followers[x]), default=0)

    filling = ("scores", "project")
    total = {True: 0.0, False: 0.0}
    for (kind, _a, _b), (engine, cost, _names) in work.items():
        if engine == "pe":
            total[kind in filling] += cost
    left, free, now_in, done = {}, {}, {}, {True: 0.0, False: 0.0}
    for x in items:
        engine = work[x[1]][0]
        free[engine], now_in[engine] = 0.0, -1
        left[engine, lap_of(x)] = left.get((engine, lap_of(x)), 0) + 1
    ready, ended, orders = {x: 0.0 for x in items if not open_[x]}, {}, {}
    for _ in items:
        best = None
        for engine, at in free.items():
            while now_in[engine] < laps and not left.get((engine, now_in[engine]), 0):
                now_in[engine] += 1
            mine = [x for x in ready if work[x[1]][0] == engine and lap_of(x) == now_in[engine]]
            if mine:
                start = max(at, min(ready[x] for x in mine))
                if best is None or start < best[0]:
                    best = start, engine, [x for x in mine if ready[x] <= start]
        start, engine, choice = best
        behind = done[True] / total[True] * total[False] <= done[False] + lead

        def urgency(x):
            return (engine == "pe" and (x[1][0] in filling) != behind, -way[x])

        x = min(choice, key=urgency)
        cost = work[x[1]][1]
        if engine == "pe":
            done[x[1][0] in filling] += cost
        del ready[x]
        free[engine] = ended[x] = start + cost
        left[engine, lap_of(x)] -= 1
        orders.setdefault((engine, lap_of(x)), []).append((*x[1], x[0] - lap_of(x)))
        for y in followers[x]:
            open_[y] -= 1
            if not open_[y]:
                ready[y] = max(ended[z] for z in after[y]) + SIGNAL + LOAD * (y[1][0] in ("scale_o", "scale_qkv"))
    return {engine: orders[engine, laps - 2] for engine in free}


def build(nc, hid, qkv_w, qkv_s, o_w, o_s, ffn_w, ffn_b, lora_b, c_in, wmod, cos_t, sin_t, ident_t,
          mask_t, spread_t, rank_t, out):
    ctx = ExitStack()
    with ctx:
        def sb(name, shape, dt):
            return ctx.enter_context(nc.sbuf_tensor(name, shape, dt))

        def sem(name):
            return ctx.enter_context(nc.semaphore(name))

        h_hi, h_lo = sb("h_hi", [P, KT, S], F32R), sb("h_lo", [P, KT, S], F32R)
        w_hi, w_lo = sb("w_hi", [P, KT, GC], F32R), sb("w_lo", [P, KT, GC], F32R)
        wo_hi, wo_lo = sb("wo_hi", [P, REP, H], F32R), sb("wo_lo", [P, REP, H], F32R)
        w_int = sb("w_int", [P, 2, GC], I32)
        w_f32 = sb("w_f32", [P, 2, GC], F32)
        q_hi, q_lo = sb("q_hi", [P, REP, S], F32R), sb("q_lo", [P, REP, S], F32R)
        k_hi, k_lo = sb("k_hi", [P, S], F32R), sb("k_lo", [P, S], F32R)
        v_hi, v_lo = sb("v_hi", [P, ST, HD], F32R), sb("v_lo", [P, ST, HD], F32R)
        prob_75 = sb("prob_75", [P, REP * 8 * P], F32)
        prob_64 = sb("prob_64", [P, REP * 7 * P], F32)
        prob_02 = sb("prob_02", [P, REP * 3 * P], F32)
        prob_13 = sb("prob_13", [P, REP * 4 * P], F32)
        prob_of = {7: prob_75, 5: prob_75, 6: prob_64, 4: prob_64, 0: prob_02, 2: prob_02, 1: prob_13, 3: prob_13}
        pt_hi, pt_lo = sb("pt_hi", [P, 2, CH], F32R), sb("pt_lo", [P, 2, CH], F32R)
        ctx_hi, ctx_lo = sb("ctx_hi", [P, 2, CH], F32R), sb("ctx_lo", [P, 2, CH], F32R)
        acc = sb("acc", [P, ST, H], F32)
        cos_s, sin_s = sb("cos_s", [P, S], F32), sb("sin_s", [P, S], F32)
        ident = sb("ident", [P, P], F32)
        ident16 = sb("ident16", [P, P], BF16)
        mask16 = sb("mask16", [P, P], BF16)
        neg_max = sb("neg_max", [P, HEAD_UNITS], F32)
        row_sum = sb("row_sum", [P, HEAD_UNITS], F32)
        inv_sum = sb("inv_sum", [P, HEAD_UNITS], F32)
        gates = sb("gates", [P, 2, H], F32)
        mod_col = sb("mod_col", [P, 4, KT], F32)
        small = sb("small", [P, 64], F32)
        parts = sb("parts", [P, ST, 6], F32)
        stats = sb("stats", [P, ST, 4], F32)

        bank = [ctx.enter_context(nc.psum_tensor(f"bank{i}", [P, 2 * CH if i < 2 else CH], F32))
                for i in range(6)]
        slots, pt_ps, ctx_ps, out_ps = bank[0:2], bank[2:4], bank[4], bank[5]

        rot_a = [prob_02[:, CH * i:CH * (i + 1)] for i in range(3)]
        rot_b = [prob_64[:, CH * i:CH * (i + 1)] for i in (5, 6)]
        v_t = w_f32[:, :, :].rearrange("p a n -> p (a n)")[:, 0:S]
        x_in = prob_75[:, :].rearrange("p (t n) -> p t n", t=ST)
        h_f32 = [prob_64[:, CH * i:CH * i + CH] for i in range(2)]
        mod_w = acc[:, :, :].rearrange("p t n -> p (t n)").rearrange("p (k n) -> p k n", k=KT)
        mod_w2 = prob_75[:, :].rearrange("p (k n) -> p k n", k=KT)

        lora_w, bias_row = prob_64[:, 1024:1536], prob_64[:, 1536:2048]
        rank, spread = prob_64[:, 2048:2112], prob_64[0:E, 2112:2240]
        r_exp, r_prob, r_tmp, *r_hot = (prob_64[:, 2240 + 64 * i:2304 + 64 * i].rearrange("p (t e) -> p t e", e=E)
                                        for i in range(5))
        logits_t = mix_t = prob_64[0:E, 2560:3584]
        mix_all, lora_f32 = prob_75[:, 0:1024], prob_75[:, 1024:2048]
        r_col = [small[:, 32 + ST * i:32 + ST * (i + 1)] for i in range(4)]

        def probs(t, h, a=0, b=None):
            width = (t + 1) * P
            b = width if b is None else b
            return prob_of[t][:, h * width + a:h * width + b]

        x_loaded = [sem(f"x_loaded{i}") for i in range(ST // 2)]
        c_loaded, mod_loaded, mod2_loaded = sem("c_loaded"), sem("mod_loaded"), sem("mod2_loaded")
        const_loaded, res_loaded, ffn_loaded = sem("const_loaded"), sem("res_loaded"), sem("ffn_loaded")
        w_loaded = [sem("w_loaded0"), sem("w_loaded1")]
        stored = sem("stored")
        ln_parts, ln_stats, ln_var, ln_rstd = sem("ln_parts"), sem("ln_stats"), sem("ln_var"), sem("ln_rstd")
        ln_normed, ln_turned = sem("ln_normed"), sem("ln_turned")
        h_affine, h_hi_done, h_lo_done = sem("h_affine"), sem("h_hi_done"), sem("h_lo_done")
        silu_exp, silu_done, silu_chain = sem("silu_exp"), sem("silu_done"), sem("silu_chain")
        mod_ps, mod_cols_done, mod_chain = sem("mod_ps"), sem("mod_cols_done"), sem("mod_chain")
        acc_zeroed, half_set = sem("acc_zeroed"), sem("half_set")
        slot_filled = sem("slot_filled")
        pt_filled = sem("pt_filled")
        pv_done = sem("pv_done")
        out_filled = sem("out_filled")
        w_scaled, w_hi_done, w_lo_done = sem("w_scaled"), sem("w_hi_done"), sem("w_lo_done")
        max_done, exp_done, inv_done, prob_done = sem("max_done"), sem("exp_done"), sem("inv_done"), sem("prob_done")
        pt_hi_done, pt_lo_done = sem("pt_hi_done"), sem("pt_lo_done")
        ctx_hi_done, ctx_lo_done = sem("ctx_hi_done"), sem("ctx_lo_done")
        acc_done = sem("acc_done")
        prob_begun = sem("prob_begun")
        rot_mul, rot_sum, rot_hi, rot_lo = sem("rot_mul"), sem("rot_sum"), sem("rot_hi"), sem("rot_lo")
        vt_copied = sem("vt_copied")
        res_chain, mixed = sem("res_chain"), sem("mixed")
        logits_t_ps, logits_t_done, logits_ps = sem("logits_t_ps"), sem("logits_t_done"), sem("logits_ps")
        router_chain, router_in, router_exp = sem("router_chain"), sem("router_in"), sem("router_exp")
        mix_done, mix_t_ps, mix_t_done = sem("mix_done"), sem("mix_t_ps"), sem("mix_t_done")
        spread_ps, spread_done, lora_ps = sem("spread_ps"), sem("spread_done"), sem("lora_ps")
        lora_mixed, lora_hi_done, lora_lo_done = sem("lora_mixed"), sem("lora_hi_done"), sem("lora_lo_done")
        b_hi_done, b_lo_done = sem("b_hi_done"), sem("b_lo_done")
        ffn_ps, ffn_chain, ffn_done = sem("ffn_ps"), sem("ffn_chain"), sem("ffn_done")

        def slot_item(n, kind, a, b=0):
            return len(SLOTS) * n + SLOTS.index((kind, a, b)) + 1

        def bank_t(n, t, kb):
            return (KEY_UNITS + VT) * n + VT + KEYS.index((t, kb)) + 1

        def bank_x(n, c):
            return (KEY_UNITS + VT) * n + c + 1

        def unit(n, t, h):
            return HEAD_UNITS * n + REP * POS[t] + h + 1

        def keys(n, t, kb):
            return KEY_UNITS * n + KEYS.index((t, kb)) + 1

        def step(n, t):
            return STEPS * n + POS[t] + 2

        def rope(n, i):
            return ROPES * n + i + 1

        def qkv_piece(n, kt):
            return (WQKV + WOUT) * n + kt + 1

        def out_piece(lap, h):
            return (WQKV + WOUT) * lap + WQKV + h + 1

        def qkv_arrived(n, kt):
            return 16 * (WQKV + WOUT) * n + 32 * (kt // 2 + 1)

        def out_arrived(lap, h):
            return 16 * (WQKV + WOUT) * lap + 16 * WQKV + 32 * (h // 2 + 1)

        def ffn_arrived(kt):
            return 16 * (WQKV + WOUT) * NKV + 16 * (kt // 2 + 1)

        def rows(i, n):
            return slice(n * i, n * (i + 1)) if isinstance(i, int) else bass.ds(i * n, n)

        def tile_of(j):
            return (k_hi[:, :], k_lo[:, :]) if j == 0 else (q_hi[:, j - 1, :], q_lo[:, j - 1, :])

        f32 = lambda ap: ap.bitcast(F32)
        order = lap_orders()

        def laps(engine, lap_work):
            with engine.Fori(0, NKV - 1) as lap:
                lap_work(lap, False)
            lap_work(NKV - 1, True)

        ln_bank = [slots[i // 2][:, (i % 2) * CH:(i % 2 + 1) * CH] for i in range(4)]
        ln_src = [x_in, acc]

        block = ctx.enter_context(nc.Block())

        @block.sync
        def _(sp):
            def piece(i, slot, weights, scales, width):
                if i is not None:
                    sp.wait_ge(w_lo_done, i - 2)
                sp.dma_start(w_int[:, slot, 0:width], weights).then_inc(w_loaded[slot], 16)
                sp.dma_start(w_f32[:, slot, 0:width], scales.to_broadcast([P, width])).then_inc(w_loaded[slot], 16)

            def qkv_pieces(n, first=False):
                for kt in range(KT):
                    piece(None if first and kt < 2 else qkv_piece(n, kt), kt % 2,
                          qkv_w[rows(n * KT + kt, P), :], qkv_s[rows(n * KT + kt, 1), :], GC)

            def out_pieces(n):
                sp.wait_ge(pt_filled, bank_x(n, VT - 1))
                for h in range(REP):
                    piece(out_piece(n, h), h % 2, o_w[rows(n * REP + h, P), :], o_s[rows(n * REP + h, 1), :], H)

            sp.dma_start(small[:, 0:KT], c_in).then_inc(c_loaded, 16)
            for i in range(ST // 2):
                sp.dma_start(x_in[:, 2 * i:2 * i + 2, :],
                             hid[2 * i * P:2 * (i + 1) * P, :].rearrange("(t p) n -> p t n", p=P)).then_inc(x_loaded[i], 16)
            sp.dma_start(mod_w, wmod[:, 0:2 * H].rearrange("(k p) n -> p k n", p=P)).then_inc(mod_loaded, 16)
            sp.dma_start(ident[:, :], ident_t).then_inc(const_loaded, 16)
            sp.dma_start(cos_s[:, :], cos_t).then_inc(const_loaded, 16)
            sp.dma_start(sin_s[:, :], sin_t).then_inc(const_loaded, 16)
            sp.dma_start(prob_64[:, 2 * CH:2 * CH + P], mask_t).then_inc(const_loaded, 16)
            qkv_pieces(0, first=True)
            sp.wait_ge(mod_ps, 1)
            sp.dma_start(mod_w, wmod[:, 2 * H:4 * H].rearrange("(k p) n -> p k n", p=P)).then_inc(mod2_loaded, 16)
            sp.wait_ge(ln_turned, 2 * KT)
            sp.dma_start(mod_w2, wmod[:, 4 * H:6 * H].rearrange("(k p) n -> p k n", p=P)).then_inc(mod2_loaded, 16)
            with sp.Fori(0, NKV - 1) as lap:
                out_pieces(lap)
                qkv_pieces(lap + 1)
            out_pieces(NKV - 1)
            for kt in range(KT):
                sp.wait_ge(w_lo_done, qkv_piece(NKV, kt) - 2)
                sp.dma_start(w_f32[:, kt % 2, :], ffn_w[kt * P:(kt + 1) * P, :]).then_inc(w_loaded[kt % 2], 16)
            sp.wait_ge(pv_done, keys(NKV - 1, ORDER[-1], ORDER[-1]))
            sp.dma_start(x_in, hid.rearrange("(t p) n -> p t n", p=P)).then_inc(res_loaded, 16)
            for dst, src in ((lora_w, lora_b), (bias_row, ffn_b.to_broadcast([P, H])), (rank, rank_t), (spread, spread_t)):
                sp.dma_start(dst, src).then_inc(ffn_loaded, 16)
            for t in range(ST):
                sp.wait_ge(ffn_done, t + 1)
                sp.dma_start(out[t * P:(t + 1) * P, :], acc[:, t, :]).then_inc(stored, 16)
            sp.wait_ge(stored, 16 * ST)

        @block.gpsimd
        def _(pool):
            def inverse_deviation(n):
                pool.wait_ge(ln_stats, ST * (n + 1))
                pool.tensor_scalar(stats[:, :, 2], stats[:, :, 1], EPS, 1.0, ALU.add, ALU.mult).then_inc(ln_var, 1)
                pool.wait_ge(ln_var, n + 1)
                pool.wait_ge(half_set, 1)
                pool.tensor_tensor(stats[:, :, 3], stats[:, :, 2], small[:, 24:24 + ST], ALU.pow).then_inc(ln_rstd, 1)

            def low_part(lo, full, hi, done):
                pool.tensor_tensor(lo, full, f32(hi), ALU.subtract).then_inc(done, 1)

            def rope_sum(n, j, c):
                i = 2 * j + c
                pool.wait_ge(rot_mul, rope(n, i))
                pool.tensor_tensor(rot_a[i % 3], rot_a[i % 3], rot_b[i % 2], ALU.add).then_inc(rot_sum, 1)

            def rope_low(n, j, c):
                hi, lo = tile_of(j)
                pool.wait_ge(rot_hi, rope(n, 2 * j + c))
                low_part(lo[:, c * CH:(c + 1) * CH], rot_a[(2 * j + c) % 3], hi[:, c * CH:(c + 1) * CH], rot_lo)

            def piece_low(hi, lo, slot, width, i):
                pool.wait_ge(w_hi_done, i)
                low_part(lo, w_f32[:, slot, 0:width], hi, w_lo_done)

            def qkv_low(n, kt):
                piece_low(w_hi[:, kt, :], w_lo[:, kt, :], kt % 2, GC, qkv_piece(n, kt))

            def normalize(n, t, h):
                u = REP * t + h
                pool.wait_ge(inv_done, unit(n, t, h))
                pool.sem_inc(prob_begun, 1)
                pool.tensor_scalar(probs(t, h), probs(t, h), inv_sum[:, u:u + 1], 1.0,
                                   ALU.mult, ALU.mult).then_inc(prob_done, 1)

            def work(n, kind, a, b):
                if kind == "norm":
                    normalize(n, a, b)
                elif kind == "rot_sum":
                    rope_sum(n, a, b)
                elif kind == "rot_low":
                    rope_low(n, a, b)
                elif kind == "low_o":
                    piece_low(wo_hi[:, a, :], wo_lo[:, a, :], a % 2, H, out_piece(n, a))
                elif kind == "low_qkv":
                    qkv_low(n, a)

            def lap_work(lap, last):
                for kind, a, b, ahead in order["pool"]:
                    if not (last and ahead) or kind == "low_qkv":
                        work(lap + ahead, kind, a, b)

            pool.memset(small[:, 24:24 + ST], -0.5).then_inc(half_set, 1)
            inverse_deviation(0)
            for kt in range(KT):
                qkv_low(0, kt)
            for kind, a, b, ahead in order["pool"]:
                if kind == "norm" and ahead and b == 0:
                    pool.wait_ge(mod_ps, 4)
                    pool.memset(acc[:, :, :], 0.0).then_inc(acc_zeroed, 1)
                if ahead and kind != "low_qkv":
                    work(0, kind, a, b)
            laps(pool, lap_work)
            pool.wait_ge(b_hi_done, 1)
            low_part(wo_lo[:, 0, :], lora_w, wo_hi[:, 0, :], b_lo_done)
            inverse_deviation(1)

        @block.scalar
        def _(act):
            def copy(dst, src, done):
                act.activation(dst, src, ACT.Copy).then_inc(done, 1)

            def affine(n):
                act.wait_ge(mod_cols_done, n + 1)
                for i in range(2 * KT):
                    kt, c = i // 2, i % 2
                    act.wait_ge(ln_turned, 2 * KT * n + i + 1)
                    if i >= 2:
                        act.wait_ge(h_lo_done, 2 * KT * n + i - 1)
                    act.activation(h_f32[i % 2], ln_bank[i % 4], ACT.Identity, bias=mod_col[:, 2 * n, kt:kt + 1],
                                   scale=mod_col[:, 2 * n + 1, kt:kt + 1]).then_inc(h_affine, 1)
                    act.wait_ge(h_affine, 2 * KT * n + i + 1)
                    copy(h_hi[:, kt, c * CH:(c + 1) * CH], h_f32[i % 2], h_hi_done)

            def qkv_high(n, kt):
                if not isinstance(n, int) or n > 0:
                    act.wait_ge(slot_filled, slot_item(n - 1, "project", PROJ - 1))
                act.wait_ge(w_scaled, qkv_piece(n, kt))
                copy(w_hi[:, kt, :], w_f32[:, kt % 2, :], w_hi_done)

            def rope_high(n, j, c):
                act.wait_ge(rot_sum, rope(n, 2 * j + c))
                copy(tile_of(j)[0][:, c * CH:(c + 1) * CH], rot_a[(2 * j + c) % 3], rot_hi)

            def values_copied(n):
                act.wait_ge(slot_filled, slot_item(n, "project", PROJ - 1))
                copy(v_t, slots[(PROJ - 1) % 2][:, :], vt_copied)

            def values_high(n, c):
                act.wait_ge(pt_filled, bank_x(n, c))
                copy(v_hi[:, REP * c:REP * (c + 1), :], pt_ps[c][:, :].rearrange("p (t d) -> p t d", d=HD), pt_hi_done)

            def exponentials(lap, t, h):
                u = REP * t + h
                act.wait_ge(max_done, unit(lap, t, h))
                act.activation(probs(t, h), slots[h % 2][:, 0:(t + 1) * P], ACT.Exp, bias=neg_max[:, u:u + 1],
                               scale=1.0, accum_out=row_sum[:, u:u + 1]).then_inc(exp_done, 1)

            def probabilities_high(n, t, kb):
                u = KEYS.index((t, kb))
                act.wait_ge(pt_filled, bank_t(n, t, kb))
                if u >= 2:
                    act.wait_ge(pv_done, keys(n, t, kb) - 2)
                copy(pt_hi[:, u % 2, :], pt_ps[u % 2][:, :], pt_hi_done)

            def output_weights_high(n, h):
                act.wait_ge(out_filled, step(n, ORDER[0]) - 1)
                act.wait_ge(w_scaled, out_piece(n, h))
                copy(wo_hi[:, h, :], w_f32[:, h % 2, 0:H], w_hi_done)

            def second_layer_high(kt):
                act.wait_ge(slot_filled, slot_item(NKV - 1, "project", PROJ - 1))
                act.wait_ge(w_loaded[kt % 2], ffn_arrived(kt))
                copy(w_hi[:, kt, :], w_f32[:, kt % 2, :], w_hi_done)

            def work(n, kind, a, b):
                if kind == "exp":
                    exponentials(n, a, b)
                elif kind == "high":
                    probabilities_high(n, a, b)
                elif kind == "ctx_high":
                    act.wait_ge(pv_done, keys(n, a, a))
                    copy(ctx_hi[:, POS[a] % 2, :], ctx_ps[:, :], ctx_hi_done)
                elif kind == "rot_high":
                    rope_high(n, a, b)
                elif kind == "v_copy":
                    values_copied(n)
                elif kind == "v_high":
                    values_high(n, a)
                elif kind == "high_o":
                    output_weights_high(n, a)
                elif kind == "high_qkv":
                    qkv_high(n, a)

            def lap_work(lap, last):
                for kind, a, b, ahead in order["act"]:
                    if last and kind == "high_qkv":
                        second_layer_high(a)
                    elif not (last and ahead):
                        work(lap + ahead, kind, a, b)

            act.wait_ge(c_loaded, 16)
            act.activation(small[:, 4:8], small[:, 0:4], ACT.Exp, scale=-1.0).then_inc(silu_exp, 1)
            act.wait_ge(const_loaded, 64)
            act.activation(ident16[:, :], ident[:, :], ACT.Copy)
            copy(mask16[:, :], prob_64[:, 2 * CH:2 * CH + P], const_loaded)
            affine(0)
            for kt in range(KT):
                qkv_high(0, kt)
            for kind, a, b, ahead in order["act"]:
                if ahead and kind != "high_qkv":
                    work(0, kind, a, b)
            act.sem_inc(ctx_hi_done, 1)
            laps(act, lap_work)

            act.wait_ge(ffn_loaded, 64)
            act.wait_ge(out_filled, step(NKV - 1, ORDER[-1]))
            copy(wo_hi[:, 0, :], lora_w, b_hi_done)
            affine(1)
            act.wait_ge(logits_t_ps, 1)
            copy(logits_t, slots[0][0:E, :], logits_t_done)
            act.wait_ge(router_in, 1)
            act.activation(r_exp, r_exp, ACT.Exp).then_inc(router_exp, 1)
            act.wait_ge(mix_t_ps, 1)
            copy(mix_t, slots[0][0:E, :], mix_t_done)
            act.wait_ge(spread_ps, 1)
            copy(mix_all, slots[1][:, :], spread_done)
            for c in range(2):
                act.wait_ge(lora_mixed, c + 1)
                copy(q_hi[:, 0, c * CH:(c + 1) * CH], lora_f32[:, c * CH:(c + 1) * CH], lora_hi_done)

        @block.vector
        def _(dve):
            def layernorm(n):
                src = ln_src[n]
                for t in range(ST):
                    dve.wait_ge(*((x_loaded[t // 2], 16) if n == 0 else (mixed, t + 1)))
                    dve.bn_stats(parts[:, t, :], src[:, t, :]).then_inc(ln_parts, 1)
                for t in range(ST):
                    dve.wait_ge(ln_parts, ST * n + t + 1)
                    dve.bn_aggr(stats[:, t, 0:2], parts[:, t, :]).then_inc(ln_stats, 1)
                dve.wait_ge(ln_stats, ST * (n + 1))
                dve.wait_ge(ln_rstd, n + 1)
                for t in range(ST):
                    dve.tensor_scalar(x_in[:, t, :], src[:, t, :], stats[:, t, 0:1], stats[:, t, 3:4],
                                      ALU.subtract, ALU.mult).then_inc(ln_normed, 1)

            def h_low(n):
                for i in range(2 * KT):
                    kt, c = i // 2, i % 2
                    dve.wait_ge(h_hi_done, 2 * KT * n + i + 1)
                    dve.tensor_tensor(h_lo[:, kt, c * CH:(c + 1) * CH], h_f32[i % 2],
                                      f32(h_hi[:, kt, c * CH:(c + 1) * CH]), ALU.subtract).then_inc(h_lo_done, 1)

            def scale_piece(slot, width, arrived):
                dve.wait_ge(w_loaded[slot], arrived)
                dve.scalar_tensor_tensor(w_f32[:, slot, 0:width], w_int[:, slot, 0:width], -ZERO,
                                         w_f32[:, slot, 0:width], ALU.add, ALU.mult).then_inc(w_scaled, 1)

            def rotate(n, j, c):
                scale = 1.0 if j == 0 else SCALE
                i, half, cols = 2 * j + c, HD // 2, slice(c * CH, (c + 1) * CH)
                a, b = rot_a[i % 3], rot_b[i % 2]
                if i == 0 and (not isinstance(n, int) or n > 0):
                    dve.wait_ge(pt_filled, bank_t(n - 1, 2, 2))
                if c == 0:
                    dve.wait_ge(slot_filled, slot_item(n, "project", j))
                if i >= 3:
                    dve.wait_ge(rot_lo, rope(n, i) - 3)
                if i >= 2:
                    dve.wait_ge(rot_sum, rope(n, i) - 2)
                ps = slots[j % 2][:, cols]
                dve.scalar_tensor_tensor(a, ps, scale, cos_s[:, cols], ALU.mult, ALU.mult)
                dve.scalar_tensor_tensor(b[0:half], ps[half:HD], scale, sin_s[0:half, cols], ALU.mult, ALU.mult)
                dve.scalar_tensor_tensor(b[half:HD], ps[0:half], scale, sin_s[half:HD, cols],
                                         ALU.mult, ALU.mult).then_inc(rot_mul, 1)

            def values_low(n, c):
                dve.wait_ge(pt_hi_done, bank_x(n, c))
                cols = slice(REP * c, REP * (c + 1))
                dve.tensor_tensor(v_lo[:, cols, :], pt_ps[c][:, :].rearrange("p (t d) -> p t d", d=HD),
                                  f32(v_hi[:, cols, :]), ALU.subtract).then_inc(pt_lo_done, 1)

            def inverse(lap, t, h):
                u = REP * t + h
                dve.wait_ge(exp_done, unit(lap, t, h))
                dve.reciprocal(inv_sum[:, u:u + 1], row_sum[:, u:u + 1]).then_inc(inv_done, 1)

            def accumulate(lap, t):
                dve.wait_ge(out_filled, step(lap, t))
                dve.tensor_tensor(acc[:, t, :], out_ps[:, :], acc[:, t, :], ALU.add).then_inc(acc_done, 1)

            def maxima(n, t, h):
                u = REP * t + h
                dve.wait_ge(slot_filled, slot_item(n, "scores", t, h))
                dve.tensor_reduce(neg_max[:, u:u + 1], slots[h % 2][:, 0:(t + 1) * P], AX.X, ALU.max,
                                  negate=True).then_inc(max_done, 1)

            def probabilities_low(n, t, kb):
                u = KEYS.index((t, kb)) % 2
                dve.wait_ge(pt_hi_done, bank_t(n, t, kb))
                dve.tensor_tensor(pt_lo[:, u, :], pt_ps[u][:, :], f32(pt_hi[:, u, :]), ALU.subtract).then_inc(pt_lo_done, 1)

            def context_low(n, t):
                u = POS[t] % 2
                dve.wait_ge(ctx_hi_done, step(n, t))
                dve.tensor_tensor(ctx_lo[:, u, :], ctx_ps[:, :], f32(ctx_hi[:, u, :]), ALU.subtract).then_inc(ctx_lo_done, 1)

            def work(n, kind, a, b):
                if kind == "max":
                    maxima(n, a, b)
                elif kind == "inverse":
                    inverse(n, a, b)
                elif kind == "low":
                    probabilities_low(n, a, b)
                elif kind == "ctx_low":
                    context_low(n, a)
                elif kind == "add":
                    accumulate(n, a)
                elif kind == "rotate":
                    rotate(n, a, b)
                elif kind == "v_low":
                    values_low(n, a)
                elif kind == "scale_o":
                    scale_piece(a % 2, H, out_arrived(n, a))
                elif kind == "scale_qkv":
                    scale_piece(a % 2, GC, qkv_arrived(n, a))

            def lap_work(lap, last):
                for kind, a, b, ahead in order["dve"]:
                    if not (last and ahead):
                        work(lap + ahead, kind, a, b)

            chained = [0]

            def link(chain, ins):
                chained[0] += 1
                ins.then_inc(chain, 1)
                dve.wait_ge(chain, chained[0])

            dve.wait_ge(silu_exp, 1)
            link(silu_chain, dve.tensor_scalar(small[:, 8:12], small[:, 4:8], 1.0, None, ALU.add))
            link(silu_chain, dve.reciprocal(small[:, 12:16], small[:, 8:12]))
            dve.tensor_tensor(small[:, 16:20], small[:, 0:4], small[:, 12:16], ALU.mult).then_inc(silu_done, 1)
            layernorm(0)
            dve.wait_ge(mod_ps, 1)
            dve.tensor_copy(mod_col[:, 0, :], ctx_ps[:, 0:KT])
            dve.tensor_scalar(mod_col[:, 1, :], ctx_ps[:, KT:2 * KT], 1.0, None, ALU.add).then_inc(mod_cols_done, 1)
            for kt in range(KT):
                scale_piece(kt % 2, GC, qkv_arrived(0, kt)) if kt < 2 else None
            h_low(0)
            for kt in range(2, KT):
                scale_piece(kt % 2, GC, qkv_arrived(0, kt))
            dve.wait_ge(const_loaded, 65)

            def second_modulation():
                dve.wait_ge(mod_ps, 2)
                dve.tensor_copy(mod_col[:, 2, :], out_ps[:, 0:KT])
                dve.tensor_scalar(mod_col[:, 3, :], out_ps[:, KT:2 * KT], 1.0, None, ALU.add).then_inc(mod_cols_done, 1)
                chained[0] = 0
                for i, ps in enumerate((ctx_ps, out_ps)):
                    gate, size = gates[:, i, :], prob_64[:, 0:H]
                    dve.wait_ge(mod_ps, 3 + i)
                    link(mod_chain, dve.tensor_scalar(gate, ps[:, :], 0.0, 2.0, ALU.is_ge, ALU.mult))
                    link(mod_chain, dve.tensor_scalar(gate, gate, -1.0, None, ALU.add))
                    link(mod_chain, dve.tensor_tensor(size, ps[:, :], gate, ALU.mult))
                    link(mod_chain, dve.scalar_tensor_tensor(gate, size, 0.25, gate, ALU.max, ALU.mult))

            for kind, a, b, ahead in order["dve"]:
                if kind == "max" and ahead and b == 0:
                    second_modulation()
                if ahead and kind != "scale_qkv":
                    work(0, kind, a, b)
            dve.wait_ge(acc_zeroed, 1)
            dve.sem_inc(acc_done, 1)
            dve.sem_inc(ctx_lo_done, 1)
            laps(dve, lap_work)

            dve.wait_ge(res_loaded, 16)
            dve.wait_ge(acc_done, step(NKV - 1, ORDER[-1]))
            for t in range(ST):
                dve.tensor_tensor(acc[:, t, :], acc[:, t, :], gates[:, 0, :], ALU.mult).then_inc(res_chain, 1)
            for t in range(ST):
                dve.wait_ge(res_chain, t + 1)
                dve.tensor_tensor(acc[:, t, :], acc[:, t, :], x_in[:, t, :], ALU.add).then_inc(mixed, 1)
            layernorm(1)
            h_low(1)

            dve.wait_ge(logits_ps, 1)
            chained[0] = 0
            wide = [P, ST, E]

            def all_experts(col):
                return col.unsqueeze(2).to_broadcast(wide)

            def routed(ins):
                link(router_chain, ins)

            logits = slots[1][:, 0:ST * E].rearrange("p (t e) -> p t e", e=E)
            routed(dve.tensor_reduce(r_col[0], logits, AX.X, ALU.max))
            dve.tensor_tensor(r_exp, logits, all_experts(r_col[0]), ALU.subtract).then_inc(router_in, 1)
            dve.wait_ge(router_exp, 1)
            routed(dve.tensor_reduce(r_col[0], r_exp, AX.X, ALU.add))
            routed(dve.reciprocal(r_col[1], r_col[0]))
            routed(dve.tensor_tensor(r_prob, r_exp, all_experts(r_col[1]), ALU.mult))
            for i in range(2):
                src, top = (r_prob, r_exp)[i], r_col[2 + i]
                routed(dve.tensor_reduce(top, src, AX.X, ALU.max))
                routed(dve.tensor_tensor(r_tmp, src, all_experts(top), ALU.is_equal))
                routed(dve.tensor_tensor(r_tmp, r_tmp, rank.rearrange("p (t e) -> p t e", e=E), ALU.mult))
                routed(dve.tensor_reduce(r_col[0], r_tmp, AX.X, ALU.max))
                routed(dve.tensor_tensor(r_hot[i], r_tmp, all_experts(r_col[0]), ALU.is_equal))
                if i == 0:
                    routed(dve.scalar_tensor_tensor(r_exp, r_hot[0], -2.0, r_prob, ALU.mult, ALU.add))
            routed(dve.tensor_tensor(r_col[0], r_col[2], r_col[3], ALU.add))
            routed(dve.reciprocal(r_col[1], r_col[0]))
            for i in range(2):
                routed(dve.tensor_tensor(r_col[2 + i], r_col[2 + i], r_col[1], ALU.mult))
                routed(dve.tensor_tensor(r_hot[i], r_hot[i], all_experts(r_col[2 + i]), ALU.mult))
            dve.tensor_tensor(r_prob, r_hot[0], r_hot[1], ALU.add).then_inc(mix_done, 1)

            dve.wait_ge(spread_done, 1)
            dve.wait_ge(lora_ps, 1)
            for c in range(2):
                cols = slice(c * CH, (c + 1) * CH)
                dve.scalar_tensor_tensor(lora_f32[:, cols], pt_ps[c][:, :], SCALING, mix_all[:, cols],
                                         ALU.mult, ALU.mult).then_inc(lora_mixed, 1)
            for c in range(2):
                cols = slice(c * CH, (c + 1) * CH)
                dve.wait_ge(lora_hi_done, c + 1)
                dve.tensor_tensor(q_lo[:, 0, cols], lora_f32[:, cols], f32(q_hi[:, 0, cols]),
                                  ALU.subtract).then_inc(lora_lo_done, 1)
            for t in range(ST):
                ps = (ctx_ps, out_ps)[t % 2]
                dve.wait_ge(ffn_ps, t + 1)
                dve.tensor_tensor(x_in[:, 4 + t % 2, :], ps[:, :], bias_row, ALU.add).then_inc(ffn_chain, 1)
                dve.wait_ge(ffn_chain, 2 * t + 1)
                dve.tensor_tensor(x_in[:, 4 + t % 2, :], x_in[:, 4 + t % 2, :], gates[:, 1, :], ALU.mult).then_inc(ffn_chain, 1)
                dve.wait_ge(ffn_chain, 2 * t + 2)
                dve.tensor_tensor(acc[:, t, :], acc[:, t, :], x_in[:, 4 + t % 2, :], ALU.add).then_inc(ffn_done, 1)

        @block.tensor
        def _(pe):
            def product(dst, left, right, start, stop):
                pe.matmul(dst, left[0], right[0], start=start, stop=False)
                pe.matmul(dst, left[0], right[1], start=False, stop=False)
                return pe.matmul(dst, left[1], right[0], start=False, stop=stop)

            def turned(n):
                for i in range(2 * KT):
                    kt, c = i // 2, i % 2
                    if i >= 4:
                        pe.wait_ge(h_affine, 2 * KT * n + i - 3)
                    for r in range(4):
                        t = 4 * c + r
                        if kt == 0:
                            pe.wait_ge(ln_normed, ST * n + t + 1)
                        mm = pe.transpose(ln_bank[i % 4][:, r * P:(r + 1) * P], x_in[:, t, kt * P:(kt + 1) * P],
                                          ident[:, :])
                    mm.then_inc(ln_turned, 1)

            silu = small[:, 16:20]

            def mod_columns(dst, weights):
                for nt in range(KT):
                    for kt in range(KT):
                        mm = pe.matmul(dst[:, nt:nt + 1], weights[:, kt, nt * P:(nt + 1) * P], silu[:, kt:kt + 1],
                                       start=kt == 0, stop=kt == KT - 1)
                return mm

            def mod_rows(dst, weights):
                for kt in range(KT):
                    mm = pe.matmul(dst, silu[:, kt:kt + 1].to_broadcast([P, P]), weights[:, kt, :],
                                   start=kt == 0, stop=kt == KT - 1)
                return mm

            def free_slot(n, kind, a, b):
                i = SLOTS.index((kind, a, b))
                was, c, d = SLOTS[i - 2]
                if i < 2 and isinstance(n, int) and n == 0:
                    pe.wait_ge(h_lo_done, 2 * KT)
                    return
                m = n if i >= 2 else n - 1
                if was == "scores":
                    pe.wait_ge(exp_done, unit(m, c, d))
                elif c < PROJ - 1:
                    pe.wait_ge(rot_mul, rope(m, 2 * c + 1))
                else:
                    pe.wait_ge(vt_copied, m + 1)

            def projection(n, j):
                free_slot(n, "project", j, 0)
                cols = slice(j * HD, (j + 1) * HD)
                for kt in range(KT):
                    if j == 0:
                        pe.wait_ge(w_lo_done, qkv_piece(n, kt))
                    a, z = kt == 0, kt == KT - 1
                    for w, h, s, e in ((w_hi, h_hi, a, False), (w_hi, h_lo, False, False), (w_lo, h_hi, False, z)):
                        for c in range(2):
                            mm = pe.matmul(slots[j % 2][:, c * CH:(c + 1) * CH], w[:, kt, cols],
                                           h[:, kt, c * CH:(c + 1) * CH], start=s, stop=e)
                mm.then_inc(slot_filled, 1)

            def values_turned(n, c):
                first = isinstance(n, int) and n == 0
                pe.wait_ge(vt_copied, n + 1)
                if not first:
                    pe.wait_ge(pt_lo_done, bank_x(n, c) - 2)
                for r in range(4):
                    mm = pe.transpose(pt_ps[c][:, r * P:(r + 1) * P], v_t[:, (4 * c + r) * P:(4 * c + r + 1) * P],
                                      ident[:, :])
                mm.then_inc(pt_filled, 1)

            def scores(n, t, h):
                free_slot(n, "scores", t, h)
                if t == ORDER[0]:
                    pe.wait_ge(rot_lo, rope(n, 2 * (h + 1) + 1))
                rows_ = slice(t * P, (t + 1) * P)
                width = (t + 1) * P
                for c in range(0, width, CH):
                    e = min(width, c + CH)
                    dst = slots[h % 2][:, c:e]
                    qh, ql, kh, kl = q_hi[:, h, rows_], q_lo[:, h, rows_], k_hi[:, c:e], k_lo[:, c:e]
                    pe.matmul(dst, qh, kh, start=True, stop=False)
                    pe.matmul(dst, qh, kl, start=False, stop=False)
                    if e == width:
                        pe.matmul(slots[h % 2][:, width - P:width], ident16[:, :], mask16[:, :], start=False, stop=False)
                    mm = pe.matmul(dst, ql, kh, start=False, stop=True)
                mm.then_inc(slot_filled, 1)

            def probabilities_turned(n, t, kb):
                u = KEYS.index((t, kb)) % 2
                if kb == 0:
                    pe.wait_ge(prob_done, unit(n, t, REP - 1))
                pe.wait_ge(pt_lo_done, bank_t(n, t, kb) - 2)
                for h in range(REP):
                    mm = pe.transpose(pt_ps[u][:, h * P:(h + 1) * P], probs(t, h, kb * P, (kb + 1) * P), ident[:, :])
                mm.then_inc(pt_filled, 1)

            def times_values(n, t, kb):
                u = KEYS.index((t, kb)) % 2
                if kb == 0:
                    pe.wait_ge(ctx_lo_done, step(n, t) - 1)
                pe.wait_ge(pt_lo_done, bank_t(n, t, kb))
                product(ctx_ps[:, :], (v_hi[:, kb, :], v_lo[:, kb, :]), (pt_hi[:, u, :], pt_lo[:, u, :]),
                        kb == 0, kb == t).then_inc(pv_done, 1)

            def output_share(n, t):
                u = POS[t] % 2
                pe.wait_ge(ctx_lo_done, step(n, t))
                pe.wait_ge(acc_done, step(n, t) - 1)
                for h in range(REP):
                    if t == ORDER[0]:
                        pe.wait_ge(w_lo_done, out_piece(n, h))
                    cols = slice(h * P, (h + 1) * P)
                    mm = product(out_ps[:, :], (ctx_hi[:, u, cols], ctx_lo[:, u, cols]),
                                 (wo_hi[:, h, :], wo_lo[:, h, :]), h == 0, h == REP - 1)
                mm.then_inc(out_filled, 1)

            def work(n, kind, a, b):
                if kind == "scores":
                    scores(n, a, b)
                elif kind == "turn":
                    probabilities_turned(n, a, b)
                elif kind == "values":
                    times_values(n, a, b)
                elif kind == "output":
                    output_share(n, a)
                elif kind == "project":
                    projection(n, a)
                elif kind == "turn_v":
                    values_turned(n, a)

            def lap_work(lap, last):
                for kind, a, b, ahead in order["pe"]:
                    if not (last and ahead):
                        work(lap + ahead, kind, a, b)

            pe.wait_ge(mod_loaded, 16)
            pe.wait_ge(silu_done, 1)
            mod_columns(ctx_ps[:, 0:KT], mod_w[:, :, 0:H])
            mod_columns(ctx_ps[:, KT:2 * KT], mod_w[:, :, H:2 * H]).then_inc(mod_ps, 1)
            pe.wait_ge(const_loaded, 65)
            turned(0)

            def second_modulation():
                pe.wait_ge(mod2_loaded, 32)
                mod_columns(out_ps[:, 0:KT], mod_w[:, :, H:2 * H])
                mod_columns(out_ps[:, KT:2 * KT], mod_w2[:, :, 0:H]).then_inc(mod_ps, 1)
                pe.wait_ge(mod_cols_done, 1)
                mod_rows(ctx_ps[:, :], mod_w[:, :, 0:H]).then_inc(mod_ps, 1)
                pe.wait_ge(mod_cols_done, 2)
                mod_rows(out_ps[:, :], mod_w2[:, :, H:2 * H]).then_inc(mod_ps, 1)

            for kind, a, b, ahead in order["pe"]:
                if kind == "scores" and ahead and b == 0:
                    second_modulation()
                if ahead:
                    work(0, kind, a, b)
            pe.sem_inc(out_filled, 1)
            pe.wait_ge(mod_chain, 7)
            laps(pe, lap_work)

            turned(1)
            pe.wait_ge(h_lo_done, 4 * KT)
            pe.wait_ge(h_affine, 4 * KT)
            pe.wait_ge(w_lo_done, qkv_piece(NKV, KT - 1))
            a_rows, r_rows = slice(H, H + ER), slice(H + ER, GC)
            for rows_, dst in ((r_rows, slots[0]), (a_rows, None)):
                for c in range(2):
                    bank_ = dst[:, c * CH:(c + 1) * CH] if dst is not None else pt_ps[c][:, :]
                    for kt in range(KT):
                        mm = product(bank_, (w_hi[:, kt, rows_], w_lo[:, kt, rows_]),
                                     (h_hi[:, kt, c * CH:(c + 1) * CH], h_lo[:, kt, c * CH:(c + 1) * CH]),
                                     kt == 0, kt == KT - 1)
                mm.then_inc(logits_t_ps if dst is not None else lora_ps, 1)
            pe.wait_ge(logits_t_done, 1)
            for t in range(ST):
                mm = pe.transpose(slots[1][:, t * E:(t + 1) * E], logits_t[:, t * P:(t + 1) * P], ident[0:E, 0:E])
            mm.then_inc(logits_ps, 1)

            def dense(t):
                pe.wait_ge(*((ffn_done, t - 1) if t >= 2 else (acc_done, step(NKV - 1, ORDER[-1]))))
                for kt in range(KT):
                    product((ctx_ps, out_ps)[t % 2][:, :], (h_hi[:, kt, t * P:(t + 1) * P], h_lo[:, kt, t * P:(t + 1) * P]),
                            (w_hi[:, kt, 0:H], w_lo[:, kt, 0:H]), kt == 0, False)

            def experts(t):
                cols = slice(t * P, (t + 1) * P)
                product((ctx_ps, out_ps)[t % 2][:, :], (q_hi[:, 0, cols], q_lo[:, 0, cols]),
                        (wo_hi[:, 0, :], wo_lo[:, 0, :]), False, True).then_inc(ffn_ps, 1)

            dense(0)
            dense(1)
            pe.wait_ge(mix_done, 1)
            for t in range(ST):
                mm = pe.transpose(slots[0][0:E, t * P:(t + 1) * P], r_prob[:, t, :], ident[:, :])
            mm.then_inc(mix_t_ps, 1)
            pe.wait_ge(mix_t_done, 1)
            for c in range(2):
                mm = pe.matmul(slots[1][:, c * CH:(c + 1) * CH], spread, mix_t[:, c * CH:(c + 1) * CH], start=True, stop=True)
            mm.then_inc(spread_ps, 1)
            pe.wait_ge(lora_lo_done, 2)
            pe.wait_ge(b_lo_done, 1)
            for t in range(ST):
                if t >= 2:
                    dense(t)
                experts(t)


def rope_tables():
    inv = (1.0 / np.float32(10000.0) ** (np.arange(0, HD, 2, dtype=np.float32) / np.float32(HD))).astype(np.float32)
    freqs = np.arange(S, dtype=np.float32)[:, None] * inv
    emb = np.concatenate([freqs, freqs], axis=-1).T
    sign = np.where(np.arange(HD) < HD // 2, -1.0, 1.0).astype(np.float32)[:, None]
    return np.cos(emb).astype(np.float32), (np.sin(emb) * sign).astype(np.float32)


def kernel(**inputs):
    import concourse.bacc as bacc
    from concourse.bass_utils import run_bass_kernel_spmd

    x = {n.removeprefix("L0_"): np.asarray(a) for n, a in inputs.items()}

    def by_group(k, q, v):
        rows = k.shape[0]
        parts = [a.reshape(rows, NKV, -1) for a in (k, q, v)]
        return np.ascontiguousarray(np.concatenate(parts, axis=2).transpose(1, 0, 2)).reshape(NKV * rows, GC)

    cos_t, sin_t = rope_tables()
    tri = np.where(np.arange(P)[None, :] > np.arange(P)[:, None], np.float32(-1e30), np.float32(0))
    arrays = {
        "hid": x["attn_hidden_states"].reshape(S, H),
        "qkv_w": by_group(x["attn_qw_k"], x["attn_qw_q"], x["attn_qw_v"]),
        "qkv_s": by_group(x["attn_scales_k"], x["attn_scales_q"], x["attn_scales_v"]),
        "o_w": x["attn_qw_o"],
        "o_s": x["attn_scales_o"],
        "ffn_w": np.concatenate([x["ffn_W_base"].T, x["ffn_A"].reshape(ER, H).T, x["ffn_W_router"].T,
                                 np.zeros((H, GC - H - ER - E), np.float32)], axis=1),
        "ffn_b": x["ffn_b_base"].reshape(1, H),
        "lora_b": x["ffn_B"].transpose(0, 2, 1).reshape(ER, H),
        "c_in": x["c"].reshape(KT, P).T,
        "wmod": x["wmod"],
        "cos_t": cos_t,
        "sin_t": sin_t,
        "ident_t": np.eye(P, dtype=np.float32),
        "mask_t": tri.astype(np.float32),
        "spread_t": np.repeat(np.eye(E, dtype=np.float32), R, axis=1),
        "rank_t": np.tile(np.arange(E, 0, -1, dtype=np.float32), (P, ST)),
    }
    nc = bacc.Bacc("TRN2", target_bir_lowering=False, num_devices=1, dynamic_dma_scratch_size=1024)
    feed, args = {}, []
    for name, a in arrays.items():
        a = np.ascontiguousarray(a)
        feed[f"in_{name}"] = a
        args.append(nc.dram_tensor(f"in_{name}", a.shape, mybir.dt.from_np(a.dtype), kind="ExternalInput").ap())
    args.append(nc.dram_tensor("out_x", (S, H), F32, kind="ExternalOutput").ap())
    build(nc, *args)
    r = run_bass_kernel_spmd(nc, [feed], core_ids=[0])
    return r.results[0]["out_x"].reshape(1, S, H)
```

```python
import math
from contextlib import ExitStack

import numpy as np

import concourse.bass as bass
import concourse.mybir as mybir
from concourse.alu_op_type import AluOpType as ALU

F32, F32R, BF16, I32 = mybir.dt.float32, mybir.dt.float32r, mybir.dt.bfloat16, mybir.dt.int32
ACT = mybir.ActivationFunctionType
AX = mybir.AxisListType

P = 128
S, H, HD = 1024, 512, 128
NKV, REP = 8, 4
KT = H // P
ST = S // P
CH = 512
GC = (REP + 2) * HD
E, R = 8, 16
ER = E * R
EPS, ZERO, SCALING = 1e-5, 8.0, 2.0
SCALE = 1.0 / math.sqrt(HD)

STEPS = ST
KEY_UNITS = STEPS * (STEPS + 1) // 2
PROJ = REP + 2
ROPES = 2 * (REP + 1)
VT = 2
WOUT, WQKV = REP, KT


ORDER = (7, 0, 6, 1, 5, 2, 4, 3)
POS = {t: i for i, t in enumerate(ORDER)}


def heads(t):
    return 1 if (t + 1) * P > CH else 2


UNITS = [(t, h) for t in ORDER for h in range(0, REP, heads(t))]
SLOTS = [("project", j, kt) for j in range(PROJ) for kt in range(KT)] + [("scores", t, h) for t, h in UNITS]
KEYS = [(t, kb) for t in ORDER for kb in range(t + 1)]
DENSE = (7, 6, 5, 4, 0, 1, 2, 3)
HALVES = (1, 0)


def columns(t):
    width = (t + 1) * P
    first = 0 if width <= CH else CH - width // 2
    return first, first + width


class Tasks(dict):

    def add(self, engine, cost, kind, a=0, b=0, after=(), release=0.0):
        self[kind, a, b] = (engine, cost, list(after), release)


def group_tasks():
    work = Tasks()

    def slot_reader(i):
        kind, a, b = SLOTS[i - 2]
        back = 0 if i >= 2 else 1
        if kind == "scores":
            return "exp", a, b, back
        return "combine" if b else "first_part", a, b, back

    work.add("dve", 0.1, "scales", 0, 0, [("combine", PROJ - 1, KT - 1, 1)])
    for kt in range(KT):
        work.add("pool", 1.0, "codes", kt, 0, [("low_o", kt + 2, 0, 1) if kt < 2 else ("codes", kt - 2, 0, 0)]
                 + [("project", PROJ - 1, kt, 1)])
    for j in range(PROJ):
        room = ("rot_low", j - 3, 1, 0) if j >= 3 else ("low_o", REP - 1, 0, 1) if j == 2 else ("rot_low", j + 3, 1, 1)
        for kt in range(KT):
            work.add("pe", 0.87, "project", j, kt, [slot_reader(SLOTS.index(("project", j, kt))), ("codes", kt, 0, 0)])
        work.add("act", 0.95, "first_part", j, 0, [("project", j, 0, 0), ("scales", 0, 0, 0), room])
        for kt in range(1, KT):
            work.add("dve", 1.17, "combine", j, kt, [("project", j, kt, 0), ("first_part", j, 0, 0)])
    for i in range(ROPES):
        j, c = i // 2, i % 2
        work.add("dve", 0.65, "rotate", j, c, [("combine", j, KT - 1, 0), ("swap", j - 1, c, 0) if j else ("turn", ORDER[0], ORDER[0], 1)])
        work.add("act", 1.15, "swap", j, c, [("rotate", j, c, 0)] + [("rot_sum", j - 1, c, 0)] * (j >= 1))
        work.add("pool", 2.6, "rot_sum", j, c, [("swap", j, c, 0)])
        work.add("act", 0.55, "rot_high", j, c, [("rot_sum", j, c, 0)])
        work.add("pool", 1.3, "rot_low", j, c, [("rot_high", j, c, 0)])
    for c in range(VT):
        work.add("pe", 0.43, "turn_v", c, 0, [("combine", PROJ - 1, KT - 1, 0), ("values", ORDER[-1], ORDER[-1], 1)])
        work.add("act", 0.55, "v_high", c, 0, [("turn_v", c, 0, 0)])
        work.add("dve", 0.62, "v_low", c, 0, [("v_high", c, 0, 0)])
    for i, (kind, t, h) in enumerate(SLOTS):
        if kind == "scores":
            p, m, (start, end) = POS[t], heads(t), columns(t)
            passes = max(256, end - start) if end <= CH else 2 * max(256, CH - start)
            room = ("turn", ORDER[p - 4], ORDER[p - 4], 0 if p >= 4 else 1)
            work.add("pe", m * (3 * passes / 2400 + 0.06), kind, t, h,
                     [slot_reader(i), ("rot_low", h + m, 1, 0), room])
            n = m * (end - start)
            work.add("dve", 0.14 + 1.04e-3 * n, "max", t, h, [("scores", t, h, 0)])
            work.add("act", 0.3 * m + 0.83e-3 * n, "exp", t, h, [("max", t, h, 0)])
            work.add("dve", 0.08, "inverse", t, h, [("exp", t, h, 0)])
            work.add("pool", 0.12 * m + 1.15e-3 * n, "norm", t, h, [("inverse", t, h, 0)])
    for i, (t, kb) in enumerate(KEYS):
        first, last, back = kb == 0, ORDER[POS[t] - 1], 0 if POS[t] else 1
        bank = ("low", *KEYS[i - 2], 0) if i >= 2 else ("v_low", i, 0, 0)
        work.add("pe", 0.43, "turn", t, kb, [bank, ("norm", t, REP - heads(t), 0)])
        work.add("act", 0.55, "high", t, kb, [("turn", t, kb, 0)] + [("values", *KEYS[i - 2], 0)] * (i >= 2))
        work.add("dve", 0.62, "low", t, kb, [("high", t, kb, 0)])
        work.add("pe", 0.65, "values", t, kb, [("low", t, kb, 0), ("v_low", 1, 0, 0)] + [("ctx_low", last, 0, back)] * first)
        if kb == t:
            work.add("act", 0.55, "ctx_high", t, 0, [("values", t, t, 0)] + [("output", ORDER[POS[t] - 2], 0, 0)] * (POS[t] >= 2))
            work.add("dve", 0.62, "ctx_low", t, 0, [("ctx_high", t, 0, 0)])
            work.add("pe", 2.6, "output", t, 0, [("ctx_low", t, 0, 0), ("low_o", REP - 1, 0, 0), ("add", last, 0, back)])
            work.add("dve", 0.62, "add", t, 0, [("output", t, 0, 0)])
    for i in range(4):
        work.add("dve", 0.62, "scale_o", i, 0, [("turn_v", 1, 0, 0)] + [("low_o", i - 2, 0, 0)] * (i >= 2))
        work.add("act", 0.55, "high_o", i, 0, [("scale_o", i, 0, 0), ("output", ORDER[-1], 0, 1)])
        work.add("pool", 1.3, "low_o", i, 0, [("high_o", i, 0, 0)])
    return work


EARLY = ("scales", "codes", "project", "first_part", "combine", "rotate", "swap", "rot_sum", "rot_high", "rot_low", "turn_v",
         "v_high", "v_low")
TOGETHER = {"project": "scores", "turn_v": "turn", "v_high": "high", "v_low": "low", "codes": "low_o",
            "high_ffn": "high_o", "low_ffn": "low_o"}
SIGNAL, LOAD = 0.1, 5.0


def early(task):
    return task[0] in EARLY or (task[0] in ("scores", "max", "exp", "inverse", "norm") and task[1] == ORDER[0])


DEPTH = (4, 2)


def layernorm_tasks(work, n, tiles, ready, arrival):
    for i, t in enumerate(tiles):
        work.add("dve", 0.62, "stats", t, n, ready(t), arrival(i))
        work.add("dve", 0.1, "aggregate", t, n, [("stats", t, n, 0)])
        work.add("pool", 0.15, "variance", t, n, [("aggregate", t, n, 0)])
        work.add("pool", 0.47, "deviation", t, n, [("variance", t, n, 0)])
        work.add("dve", 0.42, "normed", t, n, [("deviation", t, n, 0)] + [("turn", 5, 5, 0)] * n)
        d = DEPTH[n]
        bank = ("affine", tiles[i - d], n, 0) if i >= d else ("exp", *UNITS[-1], 0)
        work.add("pe", 0.43, "turn_h", t, n, [("normed", t, n, 0)] + [bank] * (i >= d or n))
        work.add("act", 1.45, "affine", t, n, [("turn_h", t, n, 0), ("mod_columns", 2 * n + 1, 0, 0)]
                 + [("h_low", tiles[i - d], n, 0)] * (i >= d))
        work.add("act", 0.55, "h_high", t, n, [("affine", t, n, 0)])
        work.add(("dve", "pool")[n], (0.62, 1.3)[n], "h_low", t, n, [("h_high", t, n, 0)])


MOD, CONSTANTS = 52.0, 20.0


def opening_tasks():
    work = Tasks()
    for task, (engine, cost, names, release) in group_tasks().items():
        if early(task):
            work[task] = (engine, cost, [x for x in names if not x[3] and x[0] != "low_o"], release)
    for kt in range(KT):
        engine, cost, names, _ = work["codes", kt, 0]
        work["codes", kt, 0] = (engine, cost, names, 24.0 + 2.0 * kt)
    layernorm_tasks(work, 0, range(ST), lambda t: [], lambda i: (9.0, 17.5, 20.8, 22.4)[i // 2])
    for kt in range(2):
        work["project", 0, kt][2].append(("h_low", ST - 1, 0, 0))
    work.add("act", 0.8, "silu_exp", 0, 0, (), 2.5)
    work.add("dve", 2.3, "silu", 0, 0, [("silu_exp", 0, 0, 0)])
    work.add("act", 0.6, "constants", 0, 0, (), CONSTANTS)
    work.add("dve", 2.6, "mod_columns", 0, 0, [("silu", 0, 0, 0)], 9.0)
    work.add("dve", 2.6, "mod_columns", 1, 0, [("silu", 0, 0, 0)], 14.0)
    for i in range(2):
        work.add("dve", 2.6, "mod_columns", 2 + i, 0, [("turn_h", ST - 1, 0, 0)], MOD)
        work.add("pe", 3.5, "mod_rows", i, 0, [("mod_columns", 1, 0, 0)], MOD)
        work.add("dve", 3.0, "gate", i, 0, [("mod_rows", i, 0, 0)])
    work.add("pool", 3.5, "zero", 0, 0, [("mod_rows", 1, 0, 0)])
    work["exp", ORDER[0], 0][2].append(("mod_columns", 3, 0, 0))
    return work


def closing_tasks():
    work = Tasks()
    for task, (engine, cost, names, release) in group_tasks().items():
        if not early(task):
            work[task] = (engine, cost, [x for x in names if not x[3] and not early(x[:3])], release)
    for kt in range(KT):
        work.add("act", 0.75, "high_ffn", kt, 0, [("low_o", 2 + kt, 0, 0) if kt < 2 else ("low_ffn", kt - 2, 0, 0)]
                 + [("mix_add", ORDER[3], 0, 0)] * (kt >= 2))
        work.add("pool", 1.9, "low_ffn", kt, 0, [("high_ffn", kt, 0, 0), ("scores", *UNITS[-1], 0)])
    for i, t in enumerate(ORDER):
        work.add("pool", 1.3, "mix_gate", t, 0, [("add", t, 0, 0)])
        work.add("pool", 1.3, "mix_add", t, 0, [("mix_gate", t, 0, 0)] + [("mix_add", ORDER[i - 4], 0, 0)] * (i >= 4))
    layernorm_tasks(work, 1, ORDER, lambda t: [("mix_add", t, 0, 0)], lambda i: 0.0)
    for t in ORDER:
        work["affine", t, 1][2].remove(("mod_columns", 3, 0, 0))
    work.add("act", 0.6, "b_high", 0, 0, [("exp", *UNITS[-1], 0), ("turn", 4, 4, 0), ("low_ffn", 1, 0, 0)])
    work.add("pool", 1.3, "b_low", 0, 0, [("b_high", 0, 0, 0)])
    work.add("pool", 1.3, "bias_gate", 0, 0, [("turn", 4, 4, 0), ("low_ffn", 1, 0, 0)])
    for t in ORDER:
        work.add("pool", 1.3, "bias", t, 0, [("bias_gate", 0, 0, 0), ("normed", t, 1, 0)])
    for i, c in enumerate(HALVES):
        h = [("h_low", t, 1, 0) for t in ORDER if t // 4 == c]
        free = [("spread_copy", HALVES[i - 1], 0, 0)] if i else [("exp", *UNITS[-1], 0)]
        work.add("pe", 2.6, "router", c, 0, h + free + [("low_ffn", KT - 1, 0, 0)])
        work.add("act", 0.7, "logits_copy", c, 0, [("router", c, 0, 0)])
        work.add("pe", 0.3, "logits_turn", c, 0, [("logits_copy", c, 0, 0)])
        work.add("dve", 0.4, "top_in", c, 0, [("logits_turn", c, 0, 0)] + [("mix_turn", HALVES[0], 0, 0)] * i)
        work.add("act", 0.3, "top_exp", c, 0, [("top_in", c, 0, 0)])
        work.add("dve", 4.2, "top", c, 0, [("top_exp", c, 0, 0)])
        work.add("pe", 0.45, "mix_turn", c, 0, [("top", c, 0, 0)])
        work.add("act", 0.7, "mix_copy", c, 0, [("mix_turn", c, 0, 0)])
        work.add("pe", 0.9, "spread", c, 0, [("mix_copy", c, 0, 0)])
        work.add("act", 0.6, "spread_copy", c, 0, [("spread", c, 0, 0)])
        work.add("pe", 2.6, "lora", c, 0, [("router", c, 0, 0)] + [("lora_mix", HALVES[0], 0, 0)] * i)
        work.add("dve", 0.62, "lora_mix", c, 0, [("lora", c, 0, 0), ("spread_copy", c, 0, 0)])
        work.add("act", 0.55, "lora_high", c, 0, [("lora_mix", c, 0, 0)])
        work.add("dve", 0.62, "lora_low", c, 0, [("lora_high", c, 0, 0)])
    for i, t in enumerate(DENSE):
        free = ("gated", DENSE[i - 4], 0, 0) if i >= 4 else ("add", ORDER[-1], 0, 0)
        work.add("pe", 2.6, "dense", t, 0, [("h_low", t, 1, 0), ("low_ffn", KT - 1, 0, 0), free])
        work.add("pe", 0.65, "experts", t, 0, [("dense", t, 0, 0), ("lora_low", t // 4, 0, 0), ("b_low", 0, 0, 0)])
        work.add("dve", 0.62, "gated", t, 0, [("experts", t, 0, 0)])
        work.add("dve", 0.62, "final", t, 0, [("gated", t, 0, 0), ("bias", t, 0, 0)])
    return work


CLOSING_FAVOUR = {"normed": -36, "turn_h": -10, "dense": -14, "final": -14, "ctx_high": 14, "add": 8, "affine": 6, "exp": -6,
                  "high": -6, "output": -4, "values": -4, "inverse": -4, "low": -2, "max": 2}


def list_schedule(work, after, lap_of, lead, favour):
    items = list(after)
    followers, waits_for = {x: [] for x in items}, {x: len(after[x]) for x in items}
    for x in items:
        for y in after[x]:
            followers[y].append(x)
    forth, count = [x for x in items if not waits_for[x]], dict(waits_for)
    for x in forth:
        for y in followers[x]:
            count[y] -= 1
            if not count[y]:
                forth.append(y)
    assert len(forth) == len(items)
    way = {}
    for x in reversed(forth):
        way[x] = work[x[1]][1] + SIGNAL + max((way[y] for y in followers[x]), default=0)

    filling = ("scores", "project")
    total, done = {True: 1e-9, False: 1e-9}, {True: 0.0, False: 0.0}
    left, free, lap_now = {}, {}, {}
    for x in items:
        engine, cost = work[x[1]][0:2]
        free[engine], lap_now[engine] = 0.0, min(lap_of(y) for y in items)
        left[engine, lap_of(x)] = left.get((engine, lap_of(x)), 0) + 1
        if engine == "pe":
            total[x[1][0] in filling] += cost
    last_lap = max(lap_of(x) for x in items)
    ready, ended, orders = {x: work[x[1]][3] for x in items if not waits_for[x]}, {}, {}
    for _ in items:
        best = None
        for engine, at in free.items():
            while lap_now[engine] < last_lap and not left.get((engine, lap_now[engine]), 0):
                lap_now[engine] += 1
            mine = [x for x in ready if work[x[1]][0] == engine and lap_of(x) == lap_now[engine]]
            if mine:
                start = max(at, min(ready[x] for x in mine))
                if best is None or start < best[0]:
                    best = start, engine, [x for x in mine if ready[x] <= start]
        start, engine, choice = best
        behind = done[True] / total[True] * total[False] <= done[False] + lead

        def urgency(x):
            return (engine == "pe" and (x[1][0] in filling) != behind, -way[x] - favour.get(x[1][0], 0))

        x = min(choice, key=urgency)
        cost = work[x[1]][1]
        if engine == "pe":
            done[x[1][0] in filling] += cost
        del ready[x]
        free[engine] = ended[x] = start + cost
        left[engine, lap_of(x)] -= 1
        orders.setdefault((engine, lap_of(x)), []).append(x)
        for y in followers[x]:
            waits_for[y] -= 1
            if not waits_for[y]:
                loaded = LOAD * (y[1][0] in ("scale_o", "scales", "codes", "high_ffn") and not work[y[1]][3])
                ready[y] = max(work[y[1]][3], max(ended[z] for z in after[y]) + SIGNAL + loaded)
    return orders


def rank(task):
    kind, a, b = task
    if kind in ("project", "scores"):
        return True, SLOTS.index(task), 0
    if kind in ("high_ffn", "low_ffn"):
        return 2, a, b
    by_step = ("scores", "max", "exp", "inverse", "norm", "turn", "high", "low", "values", "ctx_high", "ctx_low",
               "output", "add", "mix_gate", "mix_add", "bias")
    if kind in by_step or b == 1 and kind in ("stats", "aggregate", "variance", "deviation", "normed", "turn_h",
                                              "affine", "h_high", "h_low"):
        return kind not in EARLY, POS[a], b
    if kind in ("dense", "experts", "gated", "final"):
        return True, DENSE.index(a), b
    if kind in ("router", "logits_copy", "logits_turn", "top_in", "top_exp", "top", "mix_turn", "mix_copy", "spread",
                "spread_copy", "lora", "lora_mix", "lora_high", "lora_low"):
        return True, HALVES.index(a), b
    return kind not in EARLY, a, b


def in_sequence(work):
    sequences = {}
    for task in work:
        sequences.setdefault(TOGETHER.get(task[0], task[0]), []).append(task)
    for sequence in sequences.values():
        sequence.sort(key=rank)
    return sequences.values()


def lap_orders(lead=20.0, laps=3):
    work = group_tasks()
    after = {}
    for g in range(laps + 1):
        for task, (_engine, _cost, names, _release) in work.items():
            after[g, task] = {(g - back, (k, a, b)) for k, a, b, back in names if g >= back}
        for sequence in in_sequence(work):
            for i, task in enumerate(sequence):
                if i or g:
                    after[g, task].add((g if i else g - 1, sequence[i - 1]))

    def lap_of(item):
        return item[0] - 1 if early(item[1]) else item[0]

    after = {x: names for x, names in after.items() if lap_of(x) < laps}
    orders = list_schedule(work, after, lap_of, lead, {})
    return {engine: [(*task, g - lap) for g, task in orders[engine, lap]] for engine, lap in orders if lap == laps - 2}


def single_orders(work, lead, favour=None):
    after = {(0, task): {(0, x[:3]) for x in names} for task, (_e, _c, names, _r) in work.items()}
    for sequence in in_sequence(work):
        for last, task in zip(sequence, sequence[1:]):
            after[0, task].add((0, last))
    orders = list_schedule(work, after, lambda _x: 0, lead, favour or {})
    return {engine: [task for _g, task in order] for (engine, _lap), order in orders.items()}




def build(nc, hid, qkv_w, qkv_s, o_w, o_s, ffn_w, ffn_b, lora_b, c_in, wmod, cos_t, sin_t, ident_t,
          mask_t, spread_t, rank_t, c_row, mod_t, out):
    ctx = ExitStack()
    with ctx:
        def sb(name, shape, dt):
            return ctx.enter_context(nc.sbuf_tensor(name, shape, dt))

        def sem(name):
            return ctx.enter_context(nc.semaphore(name))

        h_hi, h_lo = sb("h_hi", [P, KT, S], F32R), sb("h_lo", [P, KT, S], F32R)
        w_hi = sb("w_hi", [P, KT, GC], F32R)
        wo_hi, wo_lo = sb("wo_hi", [P, REP, H], F32R), sb("wo_lo", [P, REP, H], F32R)
        w_int = sb("w_int", [P, 2, GC], I32)
        w_f32 = sb("w_f32", [P, 2, GC], F32)
        q_hi, q_lo = sb("q_hi", [P, REP, S], F32R), sb("q_lo", [P, REP, S], F32R)
        k_hi, k_lo = sb("k_hi", [P, S], F32R), sb("k_lo", [P, S], F32R)
        v_hi, v_lo = sb("v_hi", [P, ST, HD], F32R), sb("v_lo", [P, ST, HD], F32R)
        prob_75 = sb("prob_75", [P, REP * 8 * P], F32)
        prob_64 = sb("prob_64", [P, REP * 7 * P], F32)
        prob_02 = sb("prob_02", [P, REP * 3 * P], F32)
        prob_13 = sb("prob_13", [P, REP * 4 * P], F32)
        prob_of = {7: prob_75, 5: prob_75, 6: prob_64, 4: prob_64, 0: prob_02, 2: prob_02, 1: prob_13, 3: prob_13}
        proj_f32 = sb("proj_f32", [P, 2, S], F32)
        rot_b = [sb(f"rot_b{i}", [P, CH], F32)[:, :] for i in range(2)]
        scales = sb("scales", [P, PROJ * KT], F32)
        pt_hi, pt_lo = sb("pt_hi", [P, 2, CH], F32R), sb("pt_lo", [P, 2, CH], F32R)
        ctx_hi, ctx_lo = sb("ctx_hi", [P, 2, CH], F32R), sb("ctx_lo", [P, 2, CH], F32R)
        acc = sb("acc", [P, ST, H], F32)
        cos_s, sin_s = sb("cos_s", [P, S], F32), sb("sin_s", [P, S], F32)
        ident = sb("ident", [P, P], F32)
        ident16 = sb("ident16", [P, P], BF16)
        mask16 = sb("mask16", [P, P], BF16)
        neg_max = sb("neg_max", [P, STEPS * REP], F32)
        row_sum = sb("row_sum", [P, STEPS * REP], F32)
        inv_sum = sb("inv_sum", [P, STEPS * REP], F32)
        gates = sb("gates", [P, 2, H], F32)
        mod_col = sb("mod_col", [P, 4, KT], F32)
        small = sb("small", [P, 64], F32)
        parts = sb("parts", [P, ST, 6], F32)
        stats = sb("stats", [P, ST, 4], F32)

        bank = [ctx.enter_context(nc.psum_tensor(f"bank{i}", [P, 2 * CH if i < 2 else CH], F32))
                for i in range(6)]
        slots, pt_ps, ctx_ps, out_ps = bank[0:2], bank[2:4], bank[4], bank[5]

        proj_ring = [proj_f32[:, 0, :], proj_f32[:, 1, :], w_f32[:, :, :].rearrange("p a n -> p (a n)")[:, 0:S]]
        v_t = proj_ring[(PROJ - 1) % 3]
        rot_p = [prob_75[:, CH * i:CH * (i + 1)] for i in (6, 7)]
        x_in = prob_75[:, :].rearrange("p (t n) -> p t n", t=ST)
        h_f32 = [[ring[:, CH * i:CH * (i + 1)].rearrange("p (k n) -> p k n", k=KT) for i in range(DEPTH[n])]
                 for n, ring in enumerate((prob_64, w_int[:, :, :].rearrange("p a n -> p (a n)").bitcast(F32)))]
        mask_f32, gate_tmp = prob_64[:, 4 * CH:4 * CH + P], prob_64[:, 5 * CH:6 * CH]
        mod_w = acc[:, :, :].rearrange("p t n -> p (t n)").rearrange("p (k n) -> p k n", k=KT)
        acc_flat = acc[:, :, :].rearrange("p t n -> p (t n)")
        mod_wt = [acc_flat[:, 0:KT * H], acc_flat[:, KT * H:2 * KT * H], prob_64[:, 0:KT * H], prob_75[:, 0:KT * H]]
        silu_row, row_tmp = prob_13[:, 0:H], [prob_13[:, H * i:H * (i + 1)] for i in (1, 2)]

        res_ring = [table[:, CH * i:CH * (i + 1)] for table in (cos_s, sin_s) for i in range(2)]
        lora_w, bias_row = prob_64[:, 0:512], prob_64[:, 512:1024]
        rank, spread = prob_64[:, 1024:1088], prob_64[0:E, 1088:1216]
        r_exp, r_prob, r_tmp, *r_hot = (prob_64[:, 1216 + 32 * i:1248 + 32 * i].rearrange("p (t e) -> p t e", e=E)
                                        for i in range(5))
        logits_t, mix_t = prob_64[0:E, 1536:2048], prob_64[0:E, 2048:2560]
        mix_all = prob_02[:, 0:1024]
        gated_f32 = [prob_13[:, CH * i:CH * (i + 1)] for i in range(2)]
        w_lo = q_lo[:, 1:4, :].rearrange("p a n -> p (a n)").rearrange("p (k n) -> p k n", k=KT)
        b_hi, b_lo, lora_hi, lora_lo = k_hi[:, 0:H], k_lo[:, 0:H], q_hi[:, 0, :], q_lo[:, 0, :]
        r_col = [small[:, 32 + REP * i:32 + REP * (i + 1)] for i in range(4)]

        def probs(t, h, a=0, b=None):
            width = (t + 1) * P
            b = width if b is None else b
            return prob_of[t][:, h * width + a:h * width + b]

        x_loaded = [sem(f"x_loaded{i}") for i in range(ST // 2)]
        c_loaded, mod_loaded, row_loaded = sem("c_loaded"), [sem(f"mod_loaded{i}") for i in range(4)], sem("row_loaded")
        gates_loaded = sem("gates_loaded")
        ident_loaded, const_loaded, rope_loaded = sem("ident_loaded"), sem("const_loaded"), sem("rope_loaded")
        res_loaded, ffn_loaded = [sem(f"res_loaded{i}") for i in range(4)], sem("ffn_loaded")
        w_loaded = [sem("w_loaded0"), sem("w_loaded1")]
        stored = sem("stored")
        ln_parts, ln_stats, ln_var, ln_rstd = sem("ln_parts"), sem("ln_stats"), sem("ln_var"), sem("ln_rstd")
        ln_normed, ln_turned = sem("ln_normed"), sem("ln_turned")
        h_affine, h_hi_done, h_lo_done = sem("h_affine"), sem("h_hi_done"), sem("h_lo_done")
        silu_exp, silu_chain = sem("silu_exp"), sem("silu_chain")
        mod_ps, mod_cols_done, mod_chain, mod_tmp = sem("mod_ps"), sem("mod_cols_done"), sem("mod_chain"), sem("mod_tmp")
        acc_zeroed, half_set = sem("acc_zeroed"), sem("half_set")
        slot_filled = sem("slot_filled")
        pt_filled = sem("pt_filled")
        pv_done = sem("pv_done")
        out_filled = sem("out_filled")
        w_scaled, w_hi_done, w_lo_done = sem("w_scaled"), sem("w_hi_done"), sem("w_lo_done")
        max_done, exp_done, inv_done, prob_done = sem("max_done"), sem("exp_done"), sem("inv_done"), sem("prob_done")
        pt_hi_done, pt_lo_done = sem("pt_hi_done"), sem("pt_lo_done")
        ctx_hi_done, ctx_lo_done = sem("ctx_hi_done"), sem("ctx_lo_done")
        acc_done = sem("acc_done")
        prob_begun, codes_begun = sem("prob_begun"), sem("codes_begun")
        rot_mul, rot_sum, rot_hi, rot_lo = sem("rot_mul"), sem("rot_sum"), sem("rot_hi"), sem("rot_lo")
        rot_swapped, rot_cos = sem("rot_swapped"), sem("rot_cos")
        scales_loaded, scales_done = sem("scales_loaded"), sem("scales_done")
        first_done, combined = sem("first_done"), sem("combined")
        mix_gated, mixed, bias_gated, bias_added = sem("mix_gated"), sem("mixed"), sem("bias_gated"), sem("bias_added")
        logits_t_ps, logits_t_done, logits_ps = sem("logits_t_ps"), sem("logits_t_done"), sem("logits_ps")
        router_chain, router_in, router_exp = sem("router_chain"), sem("router_in"), sem("router_exp")
        mix_done, mix_t_ps, mix_t_done = sem("mix_done"), sem("mix_t_ps"), sem("mix_t_done")
        spread_ps, spread_done, lora_ps = sem("spread_ps"), sem("spread_done"), sem("lora_ps")
        lora_mixed, lora_hi_done, lora_lo_done = sem("lora_mixed"), sem("lora_hi_done"), sem("lora_lo_done")
        b_hi_done, b_lo_done = sem("b_hi_done"), sem("b_lo_done")
        ffn_ps, ffn_chain, ffn_done = sem("ffn_ps"), sem("ffn_chain"), sem("ffn_done")

        def slot_item(n, kind, a, b=0):
            return len(SLOTS) * n + SLOTS.index((kind, a, b)) + 1

        def bank_t(n, t, kb):
            return (KEY_UNITS + VT) * n + VT + KEYS.index((t, kb)) + 1

        def bank_x(n, c):
            return (KEY_UNITS + VT) * n + c + 1

        def unit(n, t, h):
            return len(UNITS) * n + UNITS.index((t, h)) + 1

        def scores_at(t, h):
            slot = slot_of("scores", t, h)
            if heads(t) == 1:
                return [slot[:, slice(*columns(t))]]
            return [slot[:, c * CH:c * CH + (t + 1) * P] for c in range(2)]

        def keys(n, t, kb):
            return KEY_UNITS * n + KEYS.index((t, kb)) + 1

        def step(n, t):
            return STEPS * n + POS[t] + 2

        def rope(n, i):
            return ROPES * n + i + 1

        def slot_of(kind, a, b):
            return slots[SLOTS.index((kind, a, b)) % 2]

        def input_part(n, j, kt):
            return PROJ * (KT - 1) * n + (KT - 1) * j + kt

        def qkv_piece(n, kt):
            return (WQKV + WOUT) * n + kt + 1

        def out_piece(lap, h):
            return (WQKV + WOUT) * lap + WQKV + h + 1

        def out_scaled(n, h):
            return REP * n + h + 1

        group_loads = 16 * (WQKV + 2 * WOUT) // 2

        def qkv_arrived(n, kt):
            return group_loads * n + 16 * (kt // 2 + 1)

        def out_arrived(lap, h):
            return group_loads * lap + 16 * WQKV // 2 + 32 * (h // 2 + 1)

        def ffn_arrived(kt):
            return qkv_arrived(NKV, kt)

        def rows(i, n):
            return slice(n * i, n * (i + 1)) if isinstance(i, int) else bass.ds(i * n, n)

        def tile_of(j):
            return (k_hi[:, :], k_lo[:, :]) if j == 0 else (q_hi[:, j - 1, :], q_lo[:, j - 1, :])

        f32 = lambda ap: ap.bitcast(F32)
        opening, lap_order = single_orders(opening_tasks(), 40.0), lap_orders()
        closing = single_orders(closing_tasks(), 36.0, CLOSING_FAVOUR)
        LAST = NKV - 1

        def laps(engine, order, work):
            with engine.Fori(0, NKV - 1) as lap:
                for kind, a, b, ahead in order:
                    work(lap + ahead, kind, a, b)

        dense_ps = [*pt_ps, ctx_ps, out_ps]

        ln_bank = [slots[i // 2][:, i % 2 * CH:(i % 2 + 1) * CH] for i in range(4)]
        ln_src = [x_in, acc]

        def place(t, n):
            return (t, POS[t])[n]

        def ln(t, n):
            return ST * n + place(t, n) + 1

        def half(c):
            return HALVES.index(c) + 1

        def half_done(c):
            return ST + 1 + max(POS[t] for t in range(4 * c, 4 * c + 4))

        block = ctx.enter_context(nc.Block())

        @block.sync
        def _(sp):
            def piece(i, slot, weights, scales_, width):
                sp.wait_ge(w_lo_done, i - 2)
                sp.dma_start(w_int[:, slot, 0:width], weights).then_inc(w_loaded[slot], 16)
                sp.dma_start(w_f32[:, slot, 0:width], scales_.to_broadcast([P, width])).then_inc(w_loaded[slot], 16)

            def qkv_pieces(n, first=False):
                for kt in range(KT):
                    if not first or kt >= 2:
                        sp.wait_ge(w_lo_done, qkv_piece(n, kt) - 2)
                    sp.dma_start(w_int[:, kt % 2, :], qkv_w[rows(n * KT + kt, P), :]).then_inc(w_loaded[kt % 2], 16)

            def load_scales(n):
                sp.dma_start(scales[:, :], qkv_s[rows(n, P), :]).then_inc(scales_loaded, 16)

            def out_pieces(n):
                sp.wait_ge(pt_filled, bank_x(n, VT - 1))
                for h in range(REP):
                    piece(out_piece(n, h), h % 2, o_w[rows(n * REP + h, P), :], o_s[rows(n * REP + h, 1), :], H)

            def mod_piece(i):
                sp.dma_start(mod_wt[i],
                             mod_t[i * P:(i + 1) * P, :]).then_inc(mod_loaded[i], 16)

            sp.dma_start(small[:, 0:KT], c_in).then_inc(c_loaded, 16)
            sp.dma_start(silu_row, c_row.to_broadcast([P, H])).then_inc(row_loaded, 16)

            def x_pair(i):
                sp.dma_start(x_in[:, 2 * i:2 * i + 2, :],
                             hid[2 * i * P:2 * (i + 1) * P, :].rearrange("(t p) n -> p t n", p=P)).then_inc(x_loaded[i], 16)

            load_scales(0)
            sp.dma_start(ident[:, :], ident_t).then_inc(ident_loaded, 16)
            x_pair(0)
            mod_piece(0)
            mod_piece(1)
            for i in range(1, ST // 2):
                x_pair(i)
            sp.dma_start(mask_f32, mask_t).then_inc(const_loaded, 16)
            qkv_pieces(0, first=True)
            sp.dma_start(cos_s[:, :], cos_t).then_inc(rope_loaded, 16)
            sp.dma_start(sin_s[:, :], sin_t).then_inc(rope_loaded, 16)
            sp.wait_ge(mod_cols_done, 2)
            sp.dma_start(mod_w, wmod.rearrange("(k p) n -> p k n", p=P)).then_inc(gates_loaded, 16)
            sp.wait_ge(h_lo_done, ST)
            mod_piece(2)
            mod_piece(3)
            with sp.Fori(0, NKV - 1) as lap:
                sp.wait_ge(combined, input_part(lap, PROJ - 1, KT - 1))
                load_scales(lap + 1)
                out_pieces(lap)
                qkv_pieces(lap + 1)

            def residual(i):
                t = ORDER[i]
                sp.dma_start(res_ring[i % 4], hid[t * P:(t + 1) * P, :]).then_inc(res_loaded[i % 4], 16)

            sp.wait_ge(rot_sum, rope(LAST, ROPES - 1))
            for i in range(4):
                residual(i)
            out_pieces(LAST)

            def second_layer_piece(kt):
                sp.wait_ge(w_lo_done, qkv_piece(NKV, kt) - 2)
                sp.dma_start(w_f32[:, kt % 2, :], ffn_w[kt * P:(kt + 1) * P, :]).then_inc(w_loaded[kt % 2], 16)

            second_layer_piece(0)
            second_layer_piece(1)
            for i in range(4, ST):
                sp.wait_ge(mixed, i - 3)
                residual(i)
            second_layer_piece(2)
            second_layer_piece(3)
            sp.wait_ge(pt_filled, bank_t(LAST, 4, 4))
            for dst, src in ((lora_w, lora_b), (bias_row, ffn_b.to_broadcast([P, H])), (rank, rank_t), (spread, spread_t)):
                sp.dma_start(dst, src).then_inc(ffn_loaded, 16)
            for i, t in enumerate(DENSE):
                sp.wait_ge(ffn_done, i + 1)
                sp.dma_start(out[t * P:(t + 1) * P, :], acc[:, t, :]).then_inc(stored, 16)
            sp.wait_ge(stored, 16 * ST)

        @block.gpsimd
        def _(pool):
            def variance(t, n):
                pool.wait_ge(ln_stats, ln(t, n))
                pool.tensor_scalar(stats[:, t, 2:3], stats[:, t, 1:2], EPS, 1.0, ALU.add, ALU.mult).then_inc(ln_var, 1)

            def deviation(t, n):
                pool.wait_ge(ln_var, ln(t, n))
                pool.tensor_tensor(stats[:, t, 3:4], stats[:, t, 2:3], small[:, 24:25], ALU.pow).then_inc(ln_rstd, 1)

            def h_low(t):
                pool.wait_ge(h_hi_done, ln(t, 1))
                cols = slice(t * P, (t + 1) * P)
                low_part(h_lo[:, :, cols], h_f32[1][POS[t] % DEPTH[1]], h_hi[:, :, cols], h_lo_done)

            def mix_gate(t):
                pool.wait_ge(acc_done, step(LAST, t))
                pool.tensor_tensor(acc[:, t, :], acc[:, t, :], gates[:, 0, :], ALU.mult).then_inc(mix_gated, 1)

            def mix_add(t):
                i = POS[t]
                pool.wait_ge(res_loaded[i % 4], 16 * (i // 4 + 1))
                pool.wait_ge(mix_gated, i + 1)
                pool.tensor_tensor(acc[:, t, :], acc[:, t, :], res_ring[i % 4], ALU.add).then_inc(mixed, 1)

            def bias_gate():
                pool.wait_ge(ffn_loaded, 64)
                pool.tensor_tensor(bias_row, bias_row, gates[:, 1, :], ALU.mult).then_inc(bias_gated, 1)

            def bias(t):
                pool.wait_ge(ln_normed, ln(t, 1))
                pool.wait_ge(bias_gated, 1)
                pool.tensor_tensor(acc[:, t, :], acc[:, t, :], bias_row, ALU.add).then_inc(bias_added, 1)

            def b_low():
                pool.wait_ge(b_hi_done, 1)
                low_part(b_lo, lora_w, b_hi, b_lo_done)

            def zero():
                pool.wait_ge(mod_ps, 2)
                pool.memset(acc[:, :, :], 0.0).then_inc(acc_zeroed, 1)

            def low_part(lo, full, hi, done):
                pool.tensor_tensor(lo, full, f32(hi), ALU.subtract).then_inc(done, 1)

            def rope_sum(n, j, c):
                i, a, cols = 2 * j + c, proj_ring[j % 3][:, c * CH:(c + 1) * CH], slice(c * CH, (c + 1) * CH)
                pool.wait_ge(rot_swapped, rope(n, i))
                pool.tensor_tensor(a, a, cos_s[:, cols], ALU.mult).then_inc(rot_cos, 1)
                pool.wait_ge(rot_cos, rope(n, i))
                pool.tensor_tensor(a, a, rot_b[i % 2], ALU.add).then_inc(rot_sum, 1)

            def rope_low(n, j, c):
                hi, lo = tile_of(j)
                cols = slice(c * CH, (c + 1) * CH)
                pool.wait_ge(rot_hi, rope(n, 2 * j + c))
                low_part(lo[:, cols], proj_ring[j % 3][:, cols], hi[:, cols], rot_lo)

            def codes(n, kt):
                if not isinstance(n, int):
                    pool.wait_ge(slot_filled, slot_item(n - 1, "project", PROJ - 1, kt))
                pool.wait_ge(w_loaded[kt % 2], qkv_arrived(n, kt))
                pool.sem_inc(codes_begun, 1)
                pool.tensor_scalar(w_hi[:, kt, :], w_int[:, kt % 2, :], -ZERO, 1.0, ALU.add, ALU.mult).then_inc(w_lo_done, 1)

            def piece_low(hi, lo, slot, width, i):
                pool.wait_ge(w_hi_done, i)
                low_part(lo, w_f32[:, slot, 0:width], hi, w_lo_done)

            def ffn_low(kt):
                pool.wait_ge(slot_filled, slot_item(LAST, "scores", *UNITS[-1]))
                piece_low(w_hi[:, kt, :], w_lo[:, kt, :], kt % 2, GC, out_scaled(NKV, kt))

            def normalize(n, t, h):
                pool.wait_ge(inv_done, unit(n, t, h))
                pool.sem_inc(prob_begun, 1)
                for g in range(h, h + heads(t)):
                    u = REP * t + g
                    ins = pool.tensor_scalar(probs(t, g), probs(t, g), inv_sum[:, u:u + 1], 1.0, ALU.mult, ALU.mult)
                ins.then_inc(prob_done, 1)

            def work(n, kind, a, b):
                if kind == "norm":
                    normalize(n, a, b)
                elif kind == "rot_sum":
                    rope_sum(n, a, b)
                elif kind == "rot_low":
                    rope_low(n, a, b)
                elif kind == "low_o":
                    piece_low(wo_hi[:, a, :], wo_lo[:, a, :], a % 2, H, out_scaled(n, a))
                elif kind == "codes":
                    codes(n, a)
                elif kind == "low_ffn":
                    ffn_low(a)
                elif kind == "variance":
                    variance(a, b)
                elif kind == "deviation":
                    deviation(a, b)
                elif kind == "h_low":
                    h_low(a)
                elif kind == "mix_gate":
                    mix_gate(a)
                elif kind == "mix_add":
                    mix_add(a)
                elif kind == "bias_gate":
                    bias_gate()
                elif kind == "bias":
                    bias(a)
                elif kind == "b_low":
                    b_low()
                elif kind == "zero":
                    zero()

            pool.memset(small[:, 24:25], -0.5).then_inc(half_set, 1)
            pool.wait_ge(half_set, 1)
            for kind, a, b in opening["pool"]:
                work(0, kind, a, b)
            laps(pool, lap_order["pool"], work)
            for kind, a, b in closing["pool"]:
                work(LAST, kind, a, b)

        @block.scalar
        def _(act):
            def copy(dst, src, done):
                act.activation(dst, src, ACT.Copy).then_inc(done, 1)

            def affine(t, n):
                i = place(t, n)
                if i == 0 and n == 1:
                    act.wait_ge(w_scaled, out_scaled(LAST, REP - 1))
                if i == 0:
                    act.wait_ge(mod_cols_done, 2 * n + 2)
                if i >= DEPTH[n]:
                    act.wait_ge(h_lo_done, ln(t, n) - DEPTH[n])
                act.wait_ge(ln_turned, ln(t, n))
                for kt in range(KT):
                    ins = act.activation(h_f32[n][i % DEPTH[n]][:, kt, :], ln_bank[i % DEPTH[n]][:, kt * P:(kt + 1) * P], ACT.Identity,
                                         bias=mod_col[:, 2 * n, kt:kt + 1], scale=mod_col[:, 2 * n + 1, kt:kt + 1])
                ins.then_inc(h_affine, 1)

            def h_high(t, n):
                act.wait_ge(h_affine, ln(t, n))
                copy(h_hi[:, :, t * P:(t + 1) * P], h_f32[n][place(t, n) % DEPTH[n]], h_hi_done)

            def constants():
                act.wait_ge(ident_loaded, 16)
                act.activation(ident16[:, :], ident[:, :], ACT.Copy)
                act.wait_ge(const_loaded, 16)
                copy(mask16[:, :], mask_f32, const_loaded)

            def silu_exponential():
                act.wait_ge(c_loaded, 16)
                act.activation(small[:, 4:8], small[:, 0:4], ACT.Exp, scale=-1.0).then_inc(silu_exp, 1)
                act.wait_ge(row_loaded, 16)
                act.activation(row_tmp[0], silu_row, ACT.Exp, scale=-1.0).then_inc(silu_exp, 1)

            def b_high():
                act.wait_ge(ffn_loaded, 64)
                act.wait_ge(slot_filled, slot_item(LAST, "scores", *UNITS[-1]))
                copy(b_hi, lora_w, b_hi_done)

            def rope_swap(n, j, c):
                i, half_ = 2 * j + c, HD // 2
                act.wait_ge(rot_mul, rope(n, i))
                if i >= 2:
                    act.wait_ge(rot_sum, rope(n, i) - 2)
                act.activation(rot_b[i % 2][0:half_], rot_p[i % 2][half_:HD], ACT.Copy)
                copy(rot_b[i % 2][half_:HD], rot_p[i % 2][0:half_], rot_swapped)

            def rope_high(n, j, c):
                act.wait_ge(rot_sum, rope(n, 2 * j + c))
                cols = slice(c * CH, (c + 1) * CH)
                copy(tile_of(j)[0][:, cols], proj_ring[j % 3][:, cols], rot_hi)

            def first_part(n, j):
                act.wait_ge(slot_filled, slot_item(n, "project", j, 0))
                act.wait_ge(scales_done, n + 1)
                if j >= 3:
                    act.wait_ge(rot_lo, rope(n, 2 * (j - 3) + 1))
                elif j == 2 and not isinstance(n, int):
                    act.wait_ge(w_lo_done, out_piece(n - 1, REP - 1))
                act.activation(proj_ring[j % 3], slot_of("project", j, 0)[:, :], ACT.Copy,
                               scale=scales[:, KT * j:KT * j + 1]).then_inc(first_done, 1)

            def values_high(n, c):
                act.wait_ge(pt_filled, bank_x(n, c))
                copy(v_hi[:, REP * c:REP * (c + 1), :], pt_ps[c][:, :].rearrange("p (t d) -> p t d", d=HD), pt_hi_done)

            def exponentials(lap, t, h):
                act.wait_ge(max_done, unit(lap, t, h))
                if isinstance(lap, int) and lap == 0 and h == 0:
                    act.wait_ge(mod_cols_done, 4)
                for i, ps in enumerate(scores_at(t, h)):
                    u = REP * t + h + i
                    ins = act.activation(probs(t, h + i), ps, ACT.Exp, bias=neg_max[:, u:u + 1],
                                         scale=1.0, accum_out=row_sum[:, u:u + 1])
                ins.then_inc(exp_done, 1)

            def probabilities_high(n, t, kb):
                u = KEYS.index((t, kb))
                act.wait_ge(pt_filled, bank_t(n, t, kb))
                if u >= 2:
                    act.wait_ge(pv_done, keys(n, t, kb) - 2)
                copy(pt_hi[:, u % 2, :], pt_ps[u % 2][:, :], pt_hi_done)

            def output_weights_high(n, h):
                act.wait_ge(out_filled, step(n, ORDER[0]) - 1)
                act.wait_ge(w_scaled, out_scaled(n, h))
                copy(wo_hi[:, h, :], w_f32[:, h % 2, 0:H], w_hi_done)

            def second_layer_high(kt):
                act.wait_ge(w_loaded[kt % 2], ffn_arrived(kt))
                copy(w_hi[:, kt, :], w_f32[:, kt % 2, :], w_hi_done)

            def work(n, kind, a, b):
                if kind == "exp":
                    exponentials(n, a, b)
                elif kind == "high":
                    probabilities_high(n, a, b)
                elif kind == "ctx_high":
                    act.wait_ge(pv_done, keys(n, a, a))
                    if POS[a] >= 2:
                        act.wait_ge(out_filled, step(n, a) - 2)
                    copy(ctx_hi[:, POS[a] % 2, :], ctx_ps[:, :], ctx_hi_done)
                elif kind == "swap":
                    rope_swap(n, a, b)
                elif kind == "rot_high":
                    rope_high(n, a, b)
                elif kind == "first_part":
                    first_part(n, a)
                elif kind == "v_high":
                    values_high(n, a)
                elif kind == "high_o":
                    output_weights_high(n, a)
                elif kind == "high_ffn":
                    second_layer_high(a)
                elif kind == "affine":
                    affine(a, b)
                elif kind == "h_high":
                    h_high(a, b)
                elif kind == "silu_exp":
                    silu_exponential()
                elif kind == "constants":
                    constants()
                elif kind == "b_high":
                    b_high()
                elif kind == "logits_copy":
                    act.wait_ge(logits_t_ps, half(a))
                    copy(logits_t, slots[1][0:E, 0:CH], logits_t_done)
                elif kind == "top_exp":
                    act.wait_ge(router_in, half(a))
                    act.activation(r_exp, r_exp, ACT.Exp).then_inc(router_exp, 1)
                elif kind == "mix_copy":
                    act.wait_ge(mix_t_ps, half(a))
                    copy(mix_t, slots[1][0:E, 0:CH], mix_t_done)
                elif kind == "spread_copy":
                    act.wait_ge(spread_ps, half(a))
                    copy(mix_all[:, a * CH:(a + 1) * CH], slots[1][:, 0:CH], spread_done)
                elif kind == "lora_high":
                    act.wait_ge(lora_mixed, half(a))
                    copy(lora_hi[:, a * CH:(a + 1) * CH], mix_all[:, a * CH:(a + 1) * CH], lora_hi_done)

            for kind, a, b in opening["act"]:
                work(0, kind, a, b)
            act.sem_inc(ctx_hi_done, 1)
            laps(act, lap_order["act"], work)
            for kind, a, b in closing["act"]:
                work(LAST, kind, a, b)

        @block.vector
        def _(dve):
            def linked(chain):
                count = [0]

                def link(ins):
                    count[0] += 1
                    ins.then_inc(chain, 1)
                    dve.wait_ge(chain, count[0])
                return link

            silu_link, gate_link, routed = linked(silu_chain), linked(mod_chain), linked(router_chain)

            def statistics(t, n):
                dve.wait_ge(*((x_loaded[t // 2], 16) if n == 0 else (mixed, POS[t] + 1)))
                dve.bn_stats(parts[:, t, :], ln_src[n][:, t, :]).then_inc(ln_parts, 1)

            def aggregate(t, n):
                dve.wait_ge(ln_parts, ln(t, n))
                dve.bn_aggr(stats[:, t, 0:2], parts[:, t, :]).then_inc(ln_stats, 1)

            def normed(t, n):
                dve.wait_ge(ln_stats, ln(t, n))
                dve.wait_ge(ln_rstd, ln(t, n))
                if n == 1:
                    dve.wait_ge(pt_filled, bank_t(LAST, 5, 5))
                dve.tensor_scalar(x_in[:, t, :], ln_src[n][:, t, :], stats[:, t, 0:1], stats[:, t, 3:4],
                                  ALU.subtract, ALU.mult).then_inc(ln_normed, 1)

            def silu():
                for i, (x, e) in enumerate(((small[:, 0:4], small[:, 4:8]), (silu_row, row_tmp[0]))):
                    y = (small[:, 16:20], silu_row)[i]
                    dve.wait_ge(silu_exp, i + 1)
                    silu_link(dve.tensor_scalar(e, e, 1.0, None, ALU.add))
                    silu_link(dve.reciprocal(e, e))
                    silu_link(dve.tensor_tensor(y, x, e, ALU.mult))

            def modulation(i):
                dve.wait_ge(mod_loaded[i], 16)
                for kt in range(KT):
                    u = KT * i + kt
                    if u >= 2:
                        dve.wait_ge(mod_tmp, u - 1)
                    weights = mod_wt[i][:, kt * H:(kt + 1) * H]
                    dve.scalar_tensor_tensor(row_tmp[u % 2], weights, 1.0, silu_row, ALU.mult, ALU.mult,
                                             accum_out=mod_col[:, i, kt:kt + 1]).then_inc(mod_tmp, 1)
                dve.wait_ge(mod_tmp, KT * (i + 1))
                dve.tensor_scalar(mod_col[:, i, :], mod_col[:, i, :], float(i % 2), None, ALU.add).then_inc(mod_cols_done, 1)

            def h_low(t):
                dve.wait_ge(h_hi_done, t + 1)
                cols = slice(t * P, (t + 1) * P)
                dve.tensor_tensor(h_lo[:, :, cols], h_f32[0][t % DEPTH[0]], f32(h_hi[:, :, cols]),
                                  ALU.subtract).then_inc(h_lo_done, 1)

            def gate(i):
                ps, gate_, size = (ctx_ps, out_ps)[i], gates[:, i, :], gate_tmp
                dve.wait_ge(mod_ps, 1 + i)
                gate_link(dve.tensor_scalar(gate_, ps[:, :], 0.0, 2.0, ALU.is_ge, ALU.mult))
                gate_link(dve.tensor_scalar(gate_, gate_, -1.0, None, ALU.add))
                gate_link(dve.tensor_tensor(size, ps[:, :], gate_, ALU.mult))
                gate_link(dve.scalar_tensor_tensor(gate_, size, 0.25, gate_, ALU.max, ALU.mult))

            def scale_piece(slot, width, arrived):
                dve.wait_ge(w_loaded[slot], arrived)
                dve.scalar_tensor_tensor(w_f32[:, slot, 0:width], w_int[:, slot, 0:width], -ZERO,
                                         w_f32[:, slot, 0:width], ALU.add, ALU.mult).then_inc(w_scaled, 1)

            def query_scales(n):
                q = scales[:, KT:KT * (REP + 1)]
                dve.wait_ge(scales_loaded, 16 * (n + 1))
                dve.tensor_scalar(q, q, SCALE, None, ALU.mult).then_inc(scales_done, 1)

            def combine(n, j, kt):
                i = KT * j + kt
                a = proj_ring[j % 3]
                dve.wait_ge(slot_filled, slot_item(n, "project", j, kt))
                dve.wait_ge(*((first_done, PROJ * n + j + 1) if kt == 1 else (combined, input_part(n, j, kt) - 1)))
                dve.scalar_tensor_tensor(a, slot_of("project", j, kt)[:, :], scales[:, i:i + 1], a,
                                         ALU.mult, ALU.add).then_inc(combined, 1)

            def rotate(n, j, c):
                i, cols = 2 * j + c, slice(c * CH, (c + 1) * CH)
                if i == 0 and isinstance(n, int):
                    dve.wait_ge(rope_loaded, 32)
                elif i == 0:
                    dve.wait_ge(pt_filled, bank_t(n - 1, 7, 7))
                dve.wait_ge(combined, input_part(n, j, KT - 1))
                if i >= 2:
                    dve.wait_ge(rot_swapped, rope(n, i) - 2)
                dve.tensor_tensor(rot_p[i % 2], proj_ring[j % 3][:, cols], sin_s[:, cols], ALU.mult).then_inc(rot_mul, 1)

            def values_low(n, c):
                dve.wait_ge(pt_hi_done, bank_x(n, c))
                cols = slice(REP * c, REP * (c + 1))
                dve.tensor_tensor(v_lo[:, cols, :], pt_ps[c][:, :].rearrange("p (t d) -> p t d", d=HD),
                                  f32(v_hi[:, cols, :]), ALU.subtract).then_inc(pt_lo_done, 1)

            def inverse(lap, t, h):
                u = REP * t + h
                dve.wait_ge(exp_done, unit(lap, t, h))
                dve.reciprocal(inv_sum[:, u:u + heads(t)], row_sum[:, u:u + heads(t)]).then_inc(inv_done, 1)

            def accumulate(lap, t):
                dve.wait_ge(out_filled, step(lap, t))
                dve.tensor_tensor(acc[:, t, :], out_ps[:, :], acc[:, t, :], ALU.add).then_inc(acc_done, 1)

            def maxima(n, t, h):
                u = REP * t + h
                dve.wait_ge(slot_filled, slot_item(n, "scores", t, h))
                if heads(t) == 1:
                    src = scores_at(t, h)[0]
                else:
                    src = slot_of("scores", t, h)[:, :].rearrange("p (c n) -> p c n", c=2)[:, :, 0:(t + 1) * P]
                dve.tensor_reduce(neg_max[:, u:u + heads(t)], src, AX.X, ALU.max, negate=True).then_inc(max_done, 1)

            def probabilities_low(n, t, kb):
                u = KEYS.index((t, kb)) % 2
                dve.wait_ge(pt_hi_done, bank_t(n, t, kb))
                dve.tensor_tensor(pt_lo[:, u, :], pt_ps[u][:, :], f32(pt_hi[:, u, :]), ALU.subtract).then_inc(pt_lo_done, 1)

            def context_low(n, t):
                u = POS[t] % 2
                dve.wait_ge(ctx_hi_done, step(n, t))
                dve.tensor_tensor(ctx_lo[:, u, :], ctx_ps[:, :], f32(ctx_hi[:, u, :]), ALU.subtract).then_inc(ctx_lo_done, 1)

            def work(n, kind, a, b):
                if kind == "max":
                    maxima(n, a, b)
                elif kind == "inverse":
                    inverse(n, a, b)
                elif kind == "low":
                    probabilities_low(n, a, b)
                elif kind == "ctx_low":
                    context_low(n, a)
                elif kind == "add":
                    accumulate(n, a)
                elif kind == "rotate":
                    rotate(n, a, b)
                elif kind == "v_low":
                    values_low(n, a)
                elif kind == "scale_o":
                    scale_piece(a % 2, H, out_arrived(n, a))
                elif kind == "scales":
                    query_scales(n)
                elif kind == "combine":
                    combine(n, a, b)
                elif kind == "silu":
                    silu()
                elif kind == "mod_columns":
                    modulation(a)
                elif kind == "gate":
                    gate(a)
                elif kind == "stats":
                    statistics(a, b)
                elif kind == "aggregate":
                    aggregate(a, b)
                elif kind == "normed":
                    normed(a, b)
                elif kind == "h_low":
                    h_low(a)
                elif kind == "top_in":
                    top_in(a)
                elif kind == "top":
                    top_two(a)
                elif kind == "lora_mix":
                    lora_mix(a)
                elif kind == "lora_low":
                    lora_low(a)
                elif kind == "gated":
                    gated(a)
                elif kind == "final":
                    final(a)

            wide = [P, REP, E]

            def all_experts(col):
                return col.unsqueeze(2).to_broadcast(wide)

            def top_in(c):
                dve.wait_ge(logits_ps, half(c))
                logits = slots[1][:, 0:REP * E].rearrange("p (t e) -> p t e", e=E)
                routed(dve.tensor_reduce(r_col[0], logits, AX.X, ALU.max))
                dve.tensor_tensor(r_exp, logits, all_experts(r_col[0]), ALU.subtract).then_inc(router_in, 1)

            def top_two(c):
                dve.wait_ge(router_exp, half(c))
                routed(dve.tensor_reduce(r_col[0], r_exp, AX.X, ALU.add))
                routed(dve.reciprocal(r_col[1], r_col[0]))
                if half(c) == 2:
                    dve.wait_ge(mix_t_ps, 1)
                routed(dve.tensor_tensor(r_prob, r_exp, all_experts(r_col[1]), ALU.mult))
                ranks = rank[:, 0:REP * E].rearrange("p (t e) -> p t e", e=E)
                for i in range(2):
                    src, top = (r_prob, r_exp)[i], r_col[2 + i]
                    routed(dve.tensor_reduce(top, src, AX.X, ALU.max))
                    routed(dve.tensor_tensor(r_tmp, src, all_experts(top), ALU.is_equal))
                    routed(dve.tensor_tensor(r_tmp, r_tmp, ranks, ALU.mult))
                    routed(dve.tensor_reduce(r_col[0], r_tmp, AX.X, ALU.max))
                    routed(dve.tensor_tensor(r_hot[i], r_tmp, all_experts(r_col[0]), ALU.is_equal))
                    if i == 0:
                        routed(dve.scalar_tensor_tensor(r_exp, r_hot[0], -2.0, r_prob, ALU.mult, ALU.add))
                routed(dve.tensor_tensor(r_col[0], r_col[2], r_col[3], ALU.add))
                routed(dve.reciprocal(r_col[1], r_col[0]))
                for i in range(2):
                    routed(dve.tensor_tensor(r_col[2 + i], r_col[2 + i], r_col[1], ALU.mult))
                    routed(dve.tensor_tensor(r_hot[i], r_hot[i], all_experts(r_col[2 + i]), ALU.mult))
                dve.tensor_tensor(r_prob, r_hot[0], r_hot[1], ALU.add).then_inc(mix_done, 1)

            def lora_mix(c):
                mix = mix_all[:, c * CH:(c + 1) * CH]
                dve.wait_ge(spread_done, half(c))
                dve.wait_ge(lora_ps, half(c))
                dve.scalar_tensor_tensor(mix, slots[1][:, CH:2 * CH], SCALING, mix, ALU.mult, ALU.mult).then_inc(lora_mixed, 1)

            def lora_low(c):
                cols = slice(c * CH, (c + 1) * CH)
                dve.wait_ge(lora_hi_done, half(c))
                dve.tensor_tensor(lora_lo[:, cols], mix_all[:, cols], f32(lora_hi[:, cols]),
                                  ALU.subtract).then_inc(lora_lo_done, 1)

            def gated(t):
                i = DENSE.index(t)
                if i >= 2:
                    dve.wait_ge(ffn_done, i - 1)
                dve.wait_ge(ffn_ps, i + 1)
                dve.tensor_tensor(gated_f32[i % 2], dense_ps[i % 4][:, :], gates[:, 1, :], ALU.mult).then_inc(ffn_chain, 1)

            def final(t):
                i = DENSE.index(t)
                dve.wait_ge(ffn_chain, i + 1)
                dve.wait_ge(bias_added, POS[t] + 1)
                dve.tensor_tensor(acc[:, t, :], acc[:, t, :], gated_f32[i % 2], ALU.add).then_inc(ffn_done, 1)

            for kind, a, b in opening["dve"]:
                work(0, kind, a, b)
            dve.wait_ge(acc_zeroed, 1)
            dve.sem_inc(acc_done, 1)
            dve.sem_inc(ctx_lo_done, 1)
            laps(dve, lap_order["dve"], work)
            for kind, a, b in closing["dve"]:
                work(LAST, kind, a, b)

        @block.tensor
        def _(pe):
            def product(dst, left, right, start, stop):
                pe.matmul(dst, left[0], right[0], start=start, stop=False)
                pe.matmul(dst, left[0], right[1], start=False, stop=False)
                return pe.matmul(dst, left[1], right[0], start=False, stop=stop)

            def normed_turned(t, n):
                i = place(t, n)
                if n == 1 and i == 0:
                    pe.wait_ge(exp_done, unit(LAST, *UNITS[-1]))
                if i >= DEPTH[n]:
                    pe.wait_ge(h_affine, ln(t, n) - DEPTH[n])
                pe.wait_ge(ln_normed, ln(t, n))
                for kt in range(KT):
                    mm = pe.transpose(ln_bank[i % DEPTH[n]][:, kt * P:(kt + 1) * P], x_in[:, t, kt * P:(kt + 1) * P], ident[:, :])
                mm.then_inc(ln_turned, 1)

            silu = small[:, 16:20]

            def free_slot(n, kind, a, b):
                i = SLOTS.index((kind, a, b))
                was, c, d = SLOTS[i - 2]
                if i < 2 and isinstance(n, int) and n == 0:
                    pe.wait_ge(h_lo_done, ST)
                    return
                m = n if i >= 2 else n - 1
                if was == "scores":
                    pe.wait_ge(exp_done, unit(m, c, d))
                elif d == 0:
                    pe.wait_ge(first_done, PROJ * m + c + 1)
                else:
                    pe.wait_ge(combined, input_part(m, c, d))

            def projection(n, j, kt):
                free_slot(n, "project", j, kt)
                if j == 0:
                    pe.wait_ge(w_lo_done, qkv_piece(n, kt))
                for h in (h_hi, h_lo):
                    for c in range(2):
                        mm = pe.matmul(slot_of("project", j, kt)[:, c * CH:(c + 1) * CH], w_hi[:, kt, j * HD:(j + 1) * HD],
                                       h[:, kt, c * CH:(c + 1) * CH], start=h is h_hi, stop=h is h_lo)
                mm.then_inc(slot_filled, 1)

            def values_turned(n, c):
                first = isinstance(n, int) and n == 0
                pe.wait_ge(combined, input_part(n, PROJ - 1, KT - 1))
                if not first:
                    pe.wait_ge(pt_lo_done, bank_x(n, c) - 2)
                for r in range(4):
                    mm = pe.transpose(pt_ps[c][:, r * P:(r + 1) * P],
                                      v_t[:, (4 * c + r) * P:(4 * c + r + 1) * P], ident[:, :])
                mm.then_inc(pt_filled, 1)

            def scores(n, t, h):
                free_slot(n, "scores", t, h)
                if isinstance(n, int) and n == 0:
                    pe.wait_ge(const_loaded, 17)
                if t == ORDER[0]:
                    pe.wait_ge(rot_lo, rope(n, 2 * (h + 1) + 1))
                rows_ = slice(t * P, (t + 1) * P)
                width = (t + 1) * P
                cut = CH - columns(t)[0] if heads(t) == 1 else width
                for i, ps in enumerate(scores_at(t, h)):
                    for c, e in ((0, cut), (cut, width)):
                        if c == e:
                            continue
                        dst = ps[:, c:e]
                        qh, ql = q_hi[:, h + i, rows_], q_lo[:, h + i, rows_]
                        pe.matmul(dst, qh, k_hi[:, c:e], start=True, stop=False)
                        pe.matmul(dst, qh, k_lo[:, c:e], start=False, stop=False)
                        if e == width:
                            pe.matmul(ps[:, width - P:width], ident16[:, :], mask16[:, :], start=False, stop=False)
                        mm = pe.matmul(dst, ql, k_hi[:, c:e], start=False, stop=True)
                mm.then_inc(slot_filled, 1)

            def probabilities_turned(n, t, kb):
                u = KEYS.index((t, kb)) % 2
                if kb == 0:
                    pe.wait_ge(prob_done, unit(n, t, REP - heads(t)))
                pe.wait_ge(pt_lo_done, bank_t(n, t, kb) - 2)
                for h in range(REP):
                    mm = pe.transpose(pt_ps[u][:, h * P:(h + 1) * P], probs(t, h, kb * P, (kb + 1) * P), ident[:, :])
                mm.then_inc(pt_filled, 1)

            def times_values(n, t, kb):
                u = KEYS.index((t, kb)) % 2
                if kb == 0:
                    pe.wait_ge(ctx_lo_done, step(n, t) - 1)
                pe.wait_ge(pt_lo_done, bank_t(n, t, kb))
                product(ctx_ps[:, :], (v_hi[:, kb, :], v_lo[:, kb, :]), (pt_hi[:, u, :], pt_lo[:, u, :]),
                        kb == 0, kb == t).then_inc(pv_done, 1)

            def output_share(n, t):
                u = POS[t] % 2
                pe.wait_ge(ctx_lo_done, step(n, t))
                pe.wait_ge(acc_done, step(n, t) - 1)
                for h in range(REP):
                    if t == ORDER[0]:
                        pe.wait_ge(w_lo_done, out_piece(n, h))
                    cols = slice(h * P, (h + 1) * P)
                    mm = product(out_ps[:, :], (ctx_hi[:, u, cols], ctx_lo[:, u, cols]),
                                 (wo_hi[:, h, :], wo_lo[:, h, :]), h == 0, h == REP - 1)
                mm.then_inc(out_filled, 1)

            def work(n, kind, a, b):
                if kind == "scores":
                    scores(n, a, b)
                elif kind == "turn":
                    probabilities_turned(n, a, b)
                elif kind == "values":
                    times_values(n, a, b)
                elif kind == "output":
                    output_share(n, a)
                elif kind == "project":
                    projection(n, a, b)
                elif kind == "turn_v":
                    values_turned(n, a)
                elif kind == "mod_rows":
                    modulation_rows(a)
                elif kind == "turn_h":
                    normed_turned(a, b)
                elif kind == "router":
                    router(a)
                elif kind == "logits_turn":
                    logits_turned(a)
                elif kind == "mix_turn":
                    mix_turned(a)
                elif kind == "spread":
                    spread_out(a)
                elif kind == "lora":
                    lora_rows(a)
                elif kind == "dense":
                    dense(a)
                elif kind == "experts":
                    experts(a)

            def modulation_rows(i):
                pe.wait_ge(gates_loaded, 16)
                pe.wait_ge(silu_chain, 3)
                for kt in range(KT):
                    mm = pe.matmul((ctx_ps, out_ps)[i][:, :], silu[:, kt:kt + 1].to_broadcast([P, P]),
                                   mod_w[:, kt, i * H:(i + 1) * H], start=kt == 0, stop=kt == KT - 1)
                mm.then_inc(mod_ps, 1)

            def rows_times_h(dst, rows_, c):
                for kt in range(KT):
                    mm = product(dst, (w_hi[:, kt, rows_], w_lo[:, kt, rows_]),
                                 (h_hi[:, kt, c * CH:(c + 1) * CH], h_lo[:, kt, c * CH:(c + 1) * CH]),
                                 kt == 0, kt == KT - 1)
                return mm

            def router(c):
                pe.wait_ge(h_lo_done, half_done(c))
                pe.wait_ge(w_lo_done, qkv_piece(NKV, KT - 1))
                if half(c) == 1:
                    pe.wait_ge(exp_done, unit(LAST, *UNITS[-1]))
                else:
                    pe.wait_ge(spread_done, 1)
                rows_times_h(slots[1][:, 0:CH], slice(H + ER, GC), c).then_inc(logits_t_ps, 1)

            def logits_turned(c):
                pe.wait_ge(logits_t_done, half(c))
                for r in range(REP):
                    mm = pe.transpose(slots[1][:, r * E:(r + 1) * E], logits_t[:, r * P:(r + 1) * P], ident[0:E, 0:E])
                mm.then_inc(logits_ps, 1)

            def mix_turned(c):
                pe.wait_ge(mix_done, half(c))
                for r in range(REP):
                    mm = pe.transpose(slots[1][0:E, r * P:(r + 1) * P], r_prob[:, r, :], ident[:, :])
                mm.then_inc(mix_t_ps, 1)

            def spread_out(c):
                pe.wait_ge(mix_t_done, half(c))
                pe.matmul(slots[1][:, 0:CH], spread, mix_t, start=True, stop=True).then_inc(spread_ps, 1)

            def lora_rows(c):
                if half(c) == 2:
                    pe.wait_ge(lora_mixed, 1)
                rows_times_h(slots[1][:, CH:2 * CH], slice(H, H + ER), c).then_inc(lora_ps, 1)

            def dense(t):
                i = DENSE.index(t)
                pe.wait_ge(*((ffn_chain, i - 3) if i >= 4 else (acc_done, step(LAST, ORDER[-1]))))
                pe.wait_ge(h_lo_done, ln(t, 1))
                pe.wait_ge(w_lo_done, qkv_piece(NKV, KT - 1))
                for kt in range(KT):
                    product(dense_ps[i % 4][:, :], (h_hi[:, kt, t * P:(t + 1) * P], h_lo[:, kt, t * P:(t + 1) * P]),
                            (w_hi[:, kt, 0:H], w_lo[:, kt, 0:H]), kt == 0, False)

            def experts(t):
                i, cols = DENSE.index(t), slice(t * P, (t + 1) * P)
                pe.wait_ge(b_lo_done, 1)
                pe.wait_ge(lora_lo_done, half(t // 4))
                product(dense_ps[i % 4][:, :], (lora_hi[:, cols], lora_lo[:, cols]), (b_hi, b_lo),
                        False, True).then_inc(ffn_ps, 1)

            pe.wait_ge(ident_loaded, 16)
            for kind, a, b in opening["pe"]:
                work(0, kind, a, b)
            pe.sem_inc(out_filled, 1)
            pe.wait_ge(mod_chain, 7)
            laps(pe, lap_order["pe"], work)
            for kind, a, b in closing["pe"]:
                work(LAST, kind, a, b)


def rope_tables():
    inv = (1.0 / np.float32(10000.0) ** (np.arange(0, HD, 2, dtype=np.float32) / np.float32(HD))).astype(np.float32)
    freqs = np.arange(S, dtype=np.float32)[:, None] * inv
    emb = np.concatenate([freqs, freqs], axis=-1).T
    sign = np.where(np.arange(HD) < HD // 2, -1.0, 1.0).astype(np.float32)[:, None]
    return np.cos(emb).astype(np.float32), np.roll((np.sin(emb) * sign).astype(np.float32), HD // 2, axis=0)


def kernel(**inputs):
    import concourse.bacc as bacc
    from concourse.bass_utils import run_bass_kernel_spmd

    x = {n.removeprefix("L0_"): np.asarray(a) for n, a in inputs.items()}

    def by_group(k, q, v):
        rows = k.shape[0]
        parts = [a.reshape(rows, NKV, -1) for a in (k, q, v)]
        return np.ascontiguousarray(np.concatenate(parts, axis=2).transpose(1, 0, 2)).reshape(NKV * rows, GC)

    cos_t, sin_t = rope_tables()
    tri = np.where(np.arange(P)[None, :] > np.arange(P)[:, None], np.float32(-1e30), np.float32(0))
    arrays = {
        "hid": x["attn_hidden_states"].reshape(S, H),
        "qkv_w": by_group(x["attn_qw_k"], x["attn_qw_q"], x["attn_qw_v"]),
        "qkv_s": by_group(x["attn_scales_k"], x["attn_scales_q"], x["attn_scales_v"])
        .reshape(NKV, KT, PROJ, P).transpose(0, 3, 2, 1).reshape(NKV * P, PROJ * KT),
        "o_w": x["attn_qw_o"],
        "o_s": x["attn_scales_o"],
        "ffn_w": np.concatenate([x["ffn_W_base"].T, x["ffn_A"].reshape(ER, H).T, x["ffn_W_router"].T,
                                 np.zeros((H, GC - H - ER - E), np.float32)], axis=1),
        "ffn_b": x["ffn_b_base"].reshape(1, H),
        "lora_b": x["ffn_B"].transpose(0, 2, 1).reshape(ER, H),
        "c_in": x["c"].reshape(KT, P).T,
        "wmod": np.concatenate([x["wmod"][:, 2 * H:3 * H], x["wmod"][:, 5 * H:6 * H]], axis=1),
        "cos_t": cos_t,
        "sin_t": sin_t,
        "ident_t": np.eye(P, dtype=np.float32),
        "mask_t": tri.astype(np.float32),
        "spread_t": np.repeat(np.eye(E, dtype=np.float32), R, axis=1),
        "rank_t": np.tile(np.arange(E, 0, -1, dtype=np.float32), (P, ST)),
        "c_row": x["c"].reshape(1, H),
        "mod_t": x["wmod"].reshape(H, 6, KT, P)[:, [0, 1, 3, 4]].transpose(1, 3, 2, 0).reshape(4 * P, KT * H),
    }
    nc = bacc.Bacc("TRN2", target_bir_lowering=False, num_devices=1, dynamic_dma_scratch_size=1024)
    feed, args = {}, []
    for name, a in arrays.items():
        a = np.ascontiguousarray(a)
        feed[f"in_{name}"] = a
        args.append(nc.dram_tensor(f"in_{name}", a.shape, mybir.dt.from_np(a.dtype), kind="ExternalInput").ap())
    args.append(nc.dram_tensor("out_x", (S, H), F32, kind="ExternalOutput").ap())
    build(nc, *args)
    r = run_bass_kernel_spmd(nc, [feed], core_ids=[0])
    return r.results[0]["out_x"].reshape(1, S, H)
```
